# Optimizing a Trainium2 kernel written in Bass

```python
import numpy as np
import jax
import jax.numpy as jnp

def _softmax(x, axis=-1):
    return jax.nn.softmax(x, axis=axis)

def _gelu(x):
    return jax.nn.gelu(x, approximate=True)

def _silu(x):
    return jax.nn.silu(x)

def _sigmoid(x):
    return jax.nn.sigmoid(x)

def _layernorm(x, axis=-1, eps=1e-05):
    m = jnp.mean(x, axis=axis, keepdims=True)
    v = jnp.var(x, axis=axis, keepdims=True)
    return (x - m) / jnp.sqrt(v + eps)

def _scatter_add(tgt, idx, src, axis=0):
    return tgt.at[idx].add(src)

def _segment_sum(src, seg, n):
    return jax.ops.segment_sum(src, seg, n)
kernel_name = 'mk_xattn_ffn_d1_seqx_r8_8fce42'

def setup_inputs(seed: int=0):
    np.random.seed(seed)
    _w = jnp.asarray

    def _rec_inputs():
        import jax
        import jax.numpy as jnp
        _rk = jax.random.key(seed)
        x = -0.0003929 + 0.9999 * jax.random.normal(jax.random.fold_in(_rk, 1), (16, 128, 128), jnp.float32)
        _lenS = 128 - jax.random.randint(jax.random.fold_in(_rk, 7), (16,), 0, max(1, 128 // 4) + 1, jnp.int32)
        _lenS2 = 120 - jax.random.randint(jax.random.fold_in(_rk, 8), (16,), 0, max(1, 120 // 4) + 1, jnp.int32)
        _ctx_1024P = jax.random.normal(jax.random.fold_in(_rk, 11), (16, 16, 128), jnp.float32)
        _ctx_1024c = jax.random.dirichlet(jax.random.fold_in(_rk, 511), 0.3 * jnp.ones((16,), jnp.float32), (16, 120))
        _ctx_1024t = jnp.einsum('bsk,bkd->bsd', _ctx_1024c, _ctx_1024P)
        _ctx_1024t = _ctx_1024t * jax.lax.rsqrt(jnp.mean(jnp.square(_ctx_1024t)) + 1e-12) * 0.953939
        ctx_1024 = 4.13588e-05 + 0.999923 * (_ctx_1024t + 0.3 * jax.random.normal(jax.random.fold_in(_rk, 611), (16, 120, 128), jnp.float32))
        return (x, ctx_1024)
    x, ctx_1024 = _rec_inputs()

    def _L0_xattn_setup():
        import jax, jax.numpy as jnp
        import numpy as np
        H = 128
        B = 8
        L_CHAR = 256
        L_SUB = 128

        def _linear(x, W, b):
            return jnp.einsum('blh,oh->blo', x, W) + b

        def _interp_linear(x, out_len):
            L_in = x.shape[1]
            pos = (jnp.arange(out_len, dtype=x.dtype) + 0.5) * (L_in / out_len) - 0.5
            pos = jnp.clip(pos, 0.0, L_in - 1)
            lo = jnp.floor(pos).astype(jnp.int32)
            hi = jnp.minimum(lo + 1, L_in - 1)
            w = (pos - lo.astype(x.dtype))[None, :, None]
            return x[:, lo] * (1 - w) + x[:, hi] * w
        key = jax.random.key(seed)
        ks = jax.random.split(key, 18)
        s = 0.02
        inp = {'char_emb': jax.random.normal(ks[0], (B, L_CHAR, H), jnp.float32), 'subword_emb': jax.random.normal(ks[1], (B, L_SUB, H), jnp.float32)}
        names = ['Wq_c', 'Wk_s', 'Wv_s', 'Wq_s', 'Wk_c', 'Wv_c']
        for i, n in enumerate(names):
            inp[n] = jax.random.normal(ks[2 + 2 * i], (H, H), jnp.float32) * s
            inp['b' + n[1:]] = jax.random.normal(ks[3 + 2 * i], (H,), jnp.float32) * s
        inp['Wg'] = jax.random.normal(ks[14], (H, 2 * H), jnp.float32) * s
        inp['bg'] = jax.random.normal(ks[15], (H,), jnp.float32) * s
        return inp
    _L0_xattn_all = _L0_xattn_setup()
    _L0_xattn_in = {k: v for k, v in _L0_xattn_all.items() if k in ('Wq_c', 'bq_c', 'Wk_s', 'bk_s', 'Wv_s', 'bv_s', 'Wq_s', 'bq_s', 'Wk_c', 'bk_c', 'Wv_c', 'bv_c', 'Wg', 'bg')}
    del _L0_xattn_all

    def _L0_ffn_setup():
        import jax, jax.numpy as jnp
        import numpy as np
        B, S, D = (2, 256, 128)
        I = 64
        E = 16
        TOP_K = 2

        def _mlp(x, wg, wu, wd):
            return jnp.einsum('bsi,id->bsd', jax.nn.silu(x @ wg) * (x @ wu), wd)
        key = jax.random.key(seed)
        ks = jax.random.split(key, 10)
        sc_d = 1.0 / np.sqrt(D)
        sc_i = 1.0 / np.sqrt(I)
        return {'x': jax.random.normal(ks[0], (B, S, D), dtype=jnp.float32), 'gate_w': jax.random.normal(ks[1], (D, E), dtype=jnp.float32) * sc_d, 'gate_b': jnp.zeros((E,), dtype=jnp.float32), 'shared_wg': jax.random.normal(ks[2], (D, I), dtype=jnp.float32) * sc_d, 'shared_wu': jax.random.normal(ks[3], (D, I), dtype=jnp.float32) * sc_d, 'shared_wd': jax.random.normal(ks[4], (I, D), dtype=jnp.float32) * sc_i, 'experts_wg': jax.random.normal(ks[5], (E, D, I), dtype=jnp.float32) * sc_d, 'experts_wu': jax.random.normal(ks[6], (E, D, I), dtype=jnp.float32) * sc_d, 'experts_wd': jax.random.normal(ks[7], (E, I, D), dtype=jnp.float32) * sc_i}
    _L0_ffn_all = _L0_ffn_setup()
    _L0_ffn_in = {k: v for k, v in _L0_ffn_all.items() if k in ('gate_w', 'gate_b', 'shared_wg', 'shared_wu', 'shared_wd', 'experts_wg', 'experts_wu', 'experts_wd')}
    del _L0_ffn_all
    return {'x': x, 'ctx_1024': ctx_1024, 'L0_xattn_Wq_c': _L0_xattn_in['Wq_c'], 'L0_xattn_bq_c': _L0_xattn_in['bq_c'], 'L0_xattn_Wk_s': _L0_xattn_in['Wk_s'], 'L0_xattn_bk_s': _L0_xattn_in['bk_s'], 'L0_xattn_Wv_s': _L0_xattn_in['Wv_s'], 'L0_xattn_bv_s': _L0_xattn_in['bv_s'], 'L0_xattn_Wq_s': _L0_xattn_in['Wq_s'], 'L0_xattn_bq_s': _L0_xattn_in['bq_s'], 'L0_xattn_Wk_c': _L0_xattn_in['Wk_c'], 'L0_xattn_bk_c': _L0_xattn_in['bk_c'], 'L0_xattn_Wv_c': _L0_xattn_in['Wv_c'], 'L0_xattn_bv_c': _L0_xattn_in['bv_c'], 'L0_xattn_Wg': _L0_xattn_in['Wg'], 'L0_xattn_bg': _L0_xattn_in['bg'], 'L0_ffn_gate_w': _L0_ffn_in['gate_w'], 'L0_ffn_gate_b': _L0_ffn_in['gate_b'], 'L0_ffn_shared_wg': _L0_ffn_in['shared_wg'], 'L0_ffn_shared_wu': _L0_ffn_in['shared_wu'], 'L0_ffn_shared_wd': _L0_ffn_in['shared_wd'], 'L0_ffn_experts_wg': _L0_ffn_in['experts_wg'], 'L0_ffn_experts_wu': _L0_ffn_in['experts_wu'], 'L0_ffn_experts_wd': _L0_ffn_in['experts_wd']}

def reference(x, ctx_1024, L0_xattn_Wq_c, L0_xattn_bq_c, L0_xattn_Wk_s, L0_xattn_bk_s, L0_xattn_Wv_s, L0_xattn_bv_s, L0_xattn_Wq_s, L0_xattn_bq_s, L0_xattn_Wk_c, L0_xattn_bk_c, L0_xattn_Wv_c, L0_xattn_bv_c, L0_xattn_Wg, L0_xattn_bg, L0_ffn_gate_w, L0_ffn_gate_b, L0_ffn_shared_wg, L0_ffn_shared_wu, L0_ffn_shared_wd, L0_ffn_experts_wg, L0_ffn_experts_wu, L0_ffn_experts_wd):
    import jax
    import jax.numpy as jnp

    def _L0_xattn_ref(char_emb, subword_emb, Wq_c, bq_c, Wk_s, bk_s, Wv_s, bv_s, Wq_s, bq_s, Wk_c, bk_c, Wv_c, bv_c, Wg, bg):
        import jax, jax.numpy as jnp
        import numpy as np
        H = 128
        B = 8
        L_CHAR = 256
        L_SUB = 128

        def _linear(x, W, b):
            return jnp.einsum('blh,oh->blo', x, W) + b

        def _interp_linear(x, out_len):
            L_in = x.shape[1]
            pos = (jnp.arange(out_len, dtype=x.dtype) + 0.5) * (L_in / out_len) - 0.5
            pos = jnp.clip(pos, 0.0, L_in - 1)
            lo = jnp.floor(pos).astype(jnp.int32)
            hi = jnp.minimum(lo + 1, L_in - 1)
            w = (pos - lo.astype(x.dtype))[None, :, None]
            return x[:, lo] * (1 - w) + x[:, hi] * w
        h = char_emb.shape[-1]
        scale = 1.0 / jnp.sqrt(jnp.asarray(h, char_emb.dtype))
        Q_char = _linear(char_emb, Wq_c, bq_c)
        K_sub = _linear(subword_emb, Wk_s, bk_s)
        V_sub = _linear(subword_emb, Wv_s, bv_s)
        scores = jnp.einsum('bqh,bkh->bqk', Q_char, K_sub) * scale
        char2sub = jnp.einsum('bqk,bkh->bqh', jax.nn.softmax(scores, axis=-1), V_sub)
        Q_sub = _linear(subword_emb, Wq_s, bq_s)
        K_char = _linear(char_emb, Wk_c, bk_c)
        V_char = _linear(char_emb, Wv_c, bv_c)
        scores2 = jnp.einsum('bqh,bkh->bqk', Q_sub, K_char) * scale
        sub2char = jnp.einsum('bqk,bkh->bqh', jax.nn.softmax(scores2, axis=-1), V_char)
        L_char = char_emb.shape[1]
        if sub2char.shape[1] != L_char:
            sub2char = _interp_linear(sub2char, L_char)
        gate_in = jnp.concatenate([char2sub, sub2char], axis=-1)
        gate = jax.nn.sigmoid(jnp.einsum('blh,oh->blo', gate_in, Wg) + bg)
        return gate * char2sub + (1 - gate) * sub2char

    def _L0_ffn_ref(x, gate_w, gate_b, shared_wg, shared_wu, shared_wd, experts_wg, experts_wu, experts_wd):
        import jax, jax.numpy as jnp
        import numpy as np
        B, S, D = (2, 256, 128)
        I = 64
        E = 16
        TOP_K = 2

        def _mlp(x, wg, wu, wd):
            return jnp.einsum('bsi,id->bsd', jax.nn.silu(x @ wg) * (x @ wu), wd)
        router_logits = jax.nn.sigmoid(x @ gate_w + gate_b)
        expert_values, expert_indices = jax.lax.top_k(router_logits, k=TOP_K)
        expert_values = expert_values / jnp.sum(expert_values, axis=-1, keepdims=True)
        hg = jnp.einsum('bsd,edi->bsei', x, experts_wg)
        hu = jnp.einsum('bsd,edi->bsei', x, experts_wu)
        all_outputs = jnp.einsum('bsei,eid->bsed', jax.nn.silu(hg) * hu, experts_wd)
        selected = jnp.take_along_axis(all_outputs, expert_indices[..., None], axis=2)
        expert_weighted = jnp.sum(expert_values[..., None] * selected, axis=2)
        return x + _mlp(x, shared_wg, shared_wu, shared_wd) + expert_weighted
    x = x + _L0_xattn_ref(_layernorm(x, axis=-1), ctx_1024, L0_xattn_Wq_c, L0_xattn_bq_c, L0_xattn_Wk_s, L0_xattn_bk_s, L0_xattn_Wv_s, L0_xattn_bv_s, L0_xattn_Wq_s, L0_xattn_bq_s, L0_xattn_Wk_c, L0_xattn_bk_c, L0_xattn_Wv_c, L0_xattn_bv_c, L0_xattn_Wg, L0_xattn_bg)
    x = x + _L0_ffn_ref(_layernorm(x, axis=-1), L0_ffn_gate_w, L0_ffn_gate_b, L0_ffn_shared_wg, L0_ffn_shared_wu, L0_ffn_shared_wd, L0_ffn_experts_wg, L0_ffn_experts_wu, L0_ffn_experts_wd)
    return x

_drawn_inputs = setup_inputs


def setup_inputs(seed=0):
    import zlib

    import numpy as np

    out = dict(_drawn_inputs(seed))
    spreads = {'L0_ffn_gate_b': (0.0, 0.1)}
    factors = {'L0_xattn_Wq_c': 8.0,
     'L0_xattn_bq_c': 8.0,
     'L0_xattn_Wk_s': 8.0,
     'L0_xattn_bk_s': 64.0,
     'L0_xattn_bv_s': 2.975,
     'L0_xattn_Wq_s': 8.0,
     'L0_xattn_bq_s': 22.309,
     'L0_xattn_Wk_c': 8.0,
     'L0_xattn_bk_c': 64.0,
     'L0_xattn_Wg': 8.0,
     'L0_xattn_bg': 8.0}
    for name, (base, spread) in spreads.items():
        noise = np.random.default_rng([zlib.crc32(name.encode()), seed]).standard_normal(out[name].shape)
        drawn = base * np.exp(spread * noise) if base else spread * noise
        out[name] = jnp.asarray(drawn.astype(out[name].dtype))
    for name, factor in factors.items():
        out[name] = (out[name] * factor).astype(out[name].dtype)
    return out
```

```python
import concourse.bass as bass
from concourse import mybir
from contextlib import ExitStack




def xattn_ffn_kernel(nc, x, ctx_in, attn_w, bias_col, bias_row, const_in, wg_in, wu_in, wsh_in, wd_in, out):
    fp32, f32r, u32 = mybir.dt.float32, mybir.dt.float32r, mybir.dt.uint32
    ALU = mybir.AluOpType
    ACT = mybir.ActivationFunctionType
    AX = mybir.AxisListType.X

    B, T, D = x.shape
    C = ctx_in.shape[1]
    GB = 2
    NG = B // GB
    N = GB * T
    E = 16
    H = 64
    CH = E * H // 128
    NF = CH + 1
    SCALE = float(D) ** -0.5
    EPS = 1e-5
    QC, KC, KS, QS = range(4)

    ctx = ExitStack()
    with ctx:
        def sb(name, shape, dt=fp32):
            return ctx.enter_context(nc.sbuf_tensor(name, shape, dt))

        def pb(name):
            return ctx.enter_context(nc.psum_tensor(name, [128, 512], fp32))

        def sem(name):
            return ctx.enter_context(nc.semaphore(name))

        aw = sb("aw", [128, 10, 128])
        bcol = sb("bcol", [128, 6])
        brow = sb("brow", [128, 3 * 128 + E])
        cst = sb("cst", [128, 2 * 128 + CH * 128 + E])
        ident = cst[:, 0:128]
        interpT = cst[:, 128:256]
        sel_f = cst[:, 256:256 + CH * 128]
        iota = cst[:, 256 + CH * 128:]
        wqk_hi = sb("wqk_hi", [128, 4, 128], f32r)
        wqk_lo = sb("wqk_lo", [128, 4, 128], f32r)
        wv = sb("wv", [128, 2, 256])
        wv_hi = sb("wv_hi", [128, 2, 256], f32r)
        wv_lo = sb("wv_lo", [128, 2, 256], f32r)
        vbias = sb("vbias", [128, 2, 256])
        wg = sb("wg", [128, E * H])
        wu = sb("wu", [128, E * H])
        wsh = sb("wsh", [128, 128])
        wg_hi = sb("wg_hi", [128, E * H], f32r)
        wg_lo = sb("wg_lo", [128, E * H], f32r)
        wu_hi = sb("wu_hi", [128, E * H], f32r)
        wu_lo = sb("wu_lo", [128, E * H], f32r)
        wsh_hi = sb("wsh_hi", [128, 128], f32r)
        wsh_lo = sb("wsh_lo", [128, 128], f32r)
        wd = sb("wd", [128, NF, 128])
        gate_w = sb("gate_w", [128, E])
        sel = sb("sel", [128, CH, 128], f32r)
        powc = sb("powc", [128, GB, 2])
        negc = sb("negc", [128, GB, 2])
        onec = sb("onec", [128, GB, 2])
        epsc = sb("epsc", [128, GB])
        halfc = sb("halfc", [128, GB])

        x_all = sb("x_all", [128, B, 128])
        ctx_t = sb("ctx_t", [128, GB, 128])
        st1 = sb("st1", [128, GB, 6])
        mv1 = sb("mv1", [128, GB, 2])
        ve1 = sb("ve1", [128, GB])
        rs1 = sb("rs1", [128, GB])
        xn = sb("xn", [128, GB, 128])
        t_hi = sb("t_hi", [128, 2, N], f32r)
        t_lo = sb("t_lo", [128, 2, N], f32r)
        qk = sb("qk", [128, 4, N])
        val = sb("val", [128, GB, 2, 256])
        mx = sb("mx", [128, GB, 2])
        nmx = sb("nmx", [128, GB, 2])
        prob = sb("prob", [128, GB, 2, 128])
        rsum = sb("rsum", [128, GB, 2])
        rinv = sb("rinv", [128, GB, 2])
        probn = sb("probn", [128, GB, 2, 128])
        pT = sb("pT", [128, GB, 2, 128])
        gt = sb("gt", [128, GB, 128])
        mixd = sb("mixd", [128, GB, 128])
        xc = sb("xc", [128, GB, 128])
        x2 = sb("x2", [128, GB, 128])
        st2 = sb("st2", [128, GB, 6])
        mv2 = sb("mv2", [128, GB, 2])
        ve2 = sb("ve2", [128, GB])
        rs2 = sb("rs2", [128, GB])
        h = sb("h", [128, GB, 128])
        x2h = sb("x2h", [128, GB, 128])
        hT_hi = sb("hT_hi", [128, N], f32r)
        hT_lo = sb("hT_lo", [128, N], f32r)
        lg = sb("lg", [128, GB, E])
        top = sb("top", [128, GB, 8])
        topi = sb("topi", [128, GB, 8], u32)
        nz = sb("nz", [128, GB, 2])
        ez = sb("ez", [128, GB, 2])
        ez1 = sb("ez1", [128, GB, 2])
        sg = sb("sg", [128, GB, 2])
        sgs = sb("sgs", [128, GB])
        sgr = sb("sgr", [128, GB])
        wt = sb("wt", [128, GB, 2])
        oh = sb("oh", [128, GB, 2, E])
        ohw = sb("ohw", [128, GB, 2, E])
        wsum = sb("wsum", [128, GB, E])
        wst = sb("wst", [128, GB, 128])
        wst_r = wst[:].bitcast(f32r)
        wT = sb("wT", [128, N], f32r)
        sil = sb("sil", [128, 2, N])
        mul = sb("mul", [128, 2, N])
        hid = sb("hid", [128, 2, N])
        hid0 = sb("hid0", [128, N])
        yout = sb("yout", [128, GB, 128])
        warm = sb("warm", [128, 2])

        GU = [pb("GU0"), pb("GU1")]
        WB = pb("WB")
        Y = pb("Y")
        BT = pb("BT")
        BQ = pb("BQ")
        BK = pb("BK")
        BV = pb("BV")
        VB = [BT, BV]

        s_aw, s_cst, s_bias, s_ffn, s_ctx, s_out = (sem(n) for n in
            ("attn_w_in", "consts_in", "bias_in", "ffn_w_in", "ctx_in_sem", "out_stored"))
        s_xin = [sem(f"x_in_{i}") for i in range(2)]
        s_zero = sem("zeros_set")
        s_pad = sem("row_padding_set")
        s_gate_w = sem("gate_w_in")
        s_qkw = sem("qk_weights_split")
        s_prod = sem("value_gate_products")
        s_wv = sem("value_weights_built")
        s_wvs = sem("value_weights_split")
        s_vb = sem("value_bias_built")
        s_fw = sem("ffn_weights_split")
        s_st1, s_mv1, s_ve1, s_rs1, s_xn = (sem(n) for n in ("stats1", "meanvar1", "vareps1", "rstd1", "xn_ready"))
        s_t, s_thi, s_tlo = sem("transposed"), sem("t_hi_ready"), sem("t_lo_ready")
        s_qk, s_qka, s_qkd = sem("qk_projected"), sem("qk_x_ready"), sem("qk_ctx_ready")
        s_s, s_mx, s_nmx, s_e, s_ri, s_pn = (sem(n) for n in
            ("scores_done", "row_max", "neg_max", "exp_done", "inv_sum", "probs_normed"))
        s_v, s_ve = sem("values_projected"), sem("values_ready")
        s_pt, s_pte = sem("probs_transposed"), sem("pT_ready")
        s_av, s_g, s_md, s_xc, s_x2 = (sem(n) for n in
            ("mix_products", "gate_tanh", "mix_diff", "mix_base", "x2_ready"))
        s_st2, s_mv2, s_ve2, s_rs2, s_h, s_x2h = (sem(n) for n in
            ("stats2", "meanvar2", "vareps2", "rstd2", "h_ready", "x2h_ready"))
        s_ht, s_hthi, s_htlo = sem("h_transposed"), sem("hT_hi_ready"), sem("hT_lo_ready")
        s_rl, s_lg, s_top, s_topi, s_nz, s_ez, s_ez1 = (sem(n) for n in
            ("router_logits", "logits_biased", "top8", "top8_index", "neg_logit", "exp_neg_logit", "one_plus_exp"))
        s_sg, s_sgs, s_sgr, s_wt, s_oh, s_ohw, s_ws, s_whi, s_wlo = (sem(n) for n in
            ("sigmoid", "sigmoid_sum", "sigmoid_inv", "top2_weights", "one_hot", "one_hot_weighted",
             "weights_row", "weights_hi", "weights_lo"))
        s_wtt, s_wT = sem("weights_transposed"), sem("wT_ready")
        s_gu, s_sil, s_mul, s_wb, s_hid, s_d = (sem(n) for n in
            ("gate_up_done", "silu_done", "mul_done", "weights_spread", "hidden_ready", "down_done"))
        s_y = sem("y_ready")
        s_waited = sem("waits_alone")

        block = ctx.enter_context(nc.Block())

        @block.sync
        def _(sp):
            sp.sem_inc(s_out, 16)
            sp.dma_start(x_all[:, 0:GB, :], x[0:GB].rearrange("b p d -> p b d")).then_inc(s_xin[0], 16)
            sp.wait_ge(s_pad, 2)
            sp.dma_start(ctx_t[0:C, :, :], ctx_in[0:GB].rearrange("b p d -> p b d")).then_inc(s_ctx, 16)
            sp.dma_start(aw[:], attn_w).then_inc(s_aw, 16)
            sp.dma_start(x_all[:, GB:B, :], x[GB:B].rearrange("b p d -> p b d")).then_inc(s_xin[1], 16)
            sp.dma_start(wg[:], wg_in).then_inc(s_ffn, 16)
            sp.dma_start(wu[:], wu_in).then_inc(s_ffn, 16)

            def load_ctx(g):
                sp.wait_ge(s_t, g)
                sp.dma_start(ctx_t[0:C, :, :],
                             ctx_in[bass.ds(g * GB, GB)].rearrange("b p d -> p b d")).then_inc(s_ctx, 16)

            def store(g):
                sp.wait_ge(s_y, g + 2)
                sp.dma_start(out[bass.ds(g * GB, GB)].rearrange("b p d -> p b d"), yout[:]).then_inc(s_out, 16)

            load_ctx(1)
            with sp.Fori(1, NG - 1) as g:
                load_ctx(g + 1)
                store(g - 1)
            store(NG - 2)
            store(NG - 1)
            sp.wait_ge(s_out, 16 * (NG + 1))

        @block.gpsimd
        def _(pool):
            nc.gpsimd.memset(halfc[:], -0.5)
            nc.gpsimd.memset(powc[:], 2.718281828459045)
            nc.gpsimd.memset(negc[:], -1.0)
            nc.gpsimd.memset(onec[:], 1.0)
            nc.gpsimd.memset(epsc[:], EPS)
            nc.gpsimd.memset(prob[:], 0.0)
            nc.gpsimd.memset(wst[:], 0.0)
            nc.gpsimd.memset(hid0[:], 0.0).then_inc(s_zero, 1)

            def inv_std(g, s_mv, mv, s_ve, ve, s_rs, rs):
                pool.wait_ge(s_mv, GB * (g + 1))
                nc.gpsimd.tensor_tensor(ve[:], mv[:, :, 1], epsc[:], ALU.add).then_inc(s_ve, 1)
                pool.wait_ge(s_ve, g + 1)
                nc.gpsimd.tensor_tensor(rs[:], ve[:], halfc[:], ALU.pow).then_inc(s_rs, 1)

            def ln1(g):
                inv_std(g, s_mv1, mv1, s_ve1, ve1, s_rs1, rs1)

            def ln2(g):
                inv_std(g, s_mv2, mv2, s_ve2, ve2, s_rs2, rs2)

            def residual(g):
                pool.wait_ge(s_x2, g + 1)
                pool.wait_ge(s_h, GB * (g + 1))
                nc.gpsimd.tensor_tensor(x2h[:], x2[:], h[:], ALU.add).then_inc(s_x2h, 1)

            def router(g):
                pool.wait_ge(s_top, GB * (g + 1))
                nc.gpsimd.tensor_tensor(nz[:], top[:, :, 0:2], negc[:], ALU.mult).then_inc(s_nz, 1)
                pool.wait_ge(s_nz, g + 1)
                nc.gpsimd.tensor_tensor(ez[:], powc[:], nz[:],
                                        ALU.pow).then_inc(s_ez, 1)
                pool.wait_ge(s_ez, g + 1)
                nc.gpsimd.tensor_tensor(ez1[:], ez[:], onec[:], ALU.add).then_inc(s_ez1, 1)

            def mix(g):
                pool.wait_ge(s_md, GB * (g + 1))
                pool.wait_ge(s_xc, GB * (g + 1))
                nc.gpsimd.tensor_tensor(x2[:], mixd[:], xc[:], ALU.add).then_inc(s_x2, 1)

            pool.wait_ge(s_zero, 1)
            ln1(0)
            pool.wait_ge(s_ffn, 16 * 6)
            for w, hi, lo in ((wsh, wsh_hi, wsh_lo), (wg, wg_hi, wg_lo), (wu, wu_hi, wu_lo)):
                nc.gpsimd.tensor_copy(hi[:], w[:]).then_inc(s_fw, 1)
            for n, (w, hi, lo) in enumerate(((wsh, wsh_hi, wsh_lo), (wg, wg_hi, wg_lo), (wu, wu_hi, wu_lo))):
                pool.wait_ge(s_fw, n + 1)
                nc.gpsimd.tensor_tensor(lo[:], w[:], hi[:].bitcast(fp32), ALU.subtract).then_inc(s_fw, 1)
            nc.gpsimd.tensor_copy(sel[:], sel_f.rearrange("p (c m) -> p c m", c=CH)).then_inc(s_fw, 1)
            ln1(1)
            mix(0)
            ln2(0)
            residual(0)
            router(0)
            with pool.Fori(1, NG - 1) as g:
                ln1(g + 1)
                mix(g)
                ln2(g)
                pool.wait_ge(s_y, g + 1)
                residual(g)
                router(g)
            g = NG - 1
            mix(g)
            ln2(g)
            pool.wait_ge(s_y, g + 1)
            residual(g)
            router(g)

        @block.scalar
        def _(act):
            act.dma_start(bcol[:], bias_col).then_inc(s_bias, 16)
            act.dma_start(brow[:], bias_row.partition_broadcast(128)).then_inc(s_bias, 16)
            act.dma_start(cst[:], const_in).then_inc(s_cst, 16)
            act.dma_start(wsh[:], wsh_in[:, 0:128]).then_inc(s_ffn, 16)
            act.dma_start(gate_w[:], wsh_in[:, 128:128 + E]).then_inc(s_ffn, 16)
            act.dma_start(wd[0:64, 0, :], wd_in[0:64, :]).then_inc(s_ffn, 16)
            act.dma_start(wd[:, 1:NF, :], wd_in[64:64 + CH * 128, :].rearrange("(c p) d -> p c d", p=128)).then_inc(s_ffn, 16)

            def t_split(g):
                act.wait_ge(s_t, g + 1)
                nc.scalar.activation(t_hi[:].rearrange("p s n -> p (s n)"), BT[:], ACT.Copy).then_inc(s_thi, 1)

            def qk_bias(g):
                act.wait_ge(s_qk, 2 * g + 1)
                for n in (QC, KC):
                    nc.scalar.activation(qk[:, n, :], BQ[:, n * N:(n + 1) * N], ACT.Identity,
                                         bias=bcol[:, n:n + 1]).then_inc(s_qka, 1)

            def exps(g):
                act.wait_ge(s_nmx, g + 1)
                for b in range(GB):
                    for side, k in ((0, C), (1, 128)):
                        nc.scalar.activation(prob[:, b, side, 0:k], BQ[:, (2 * b + side) * 128:(2 * b + side) * 128 + k],
                                             ACT.Exp, bias=nmx[:, b, side:side + 1], scale=SCALE,
                                             accum_out=rsum[:, b, side:side + 1]).then_inc(s_e, 1)

            def pt_copy(g):
                act.wait_ge(s_pt, g + 1)
                nc.scalar.activation(pT[:].rearrange("p b s n -> p (b s n)"), BK[:], ACT.Copy).then_inc(s_pte, 1)

            def gate(g):
                for b in range(GB):
                    act.wait_ge(s_av, GB * g + b + 1)
                    nc.scalar.activation(gt[:, b, :], VB[b][:, 128:256], ACT.Tanh, scale=-0.5).then_inc(s_g, 1)

            def ht_split(g):
                act.wait_ge(s_ht, g + 1)
                nc.scalar.activation(hT_hi[:], BQ[:, 0:N], ACT.Copy).then_inc(s_hthi, 1)

            def silu(g, c):
                act.wait_ge(s_gu, NF * g + c + 1)
                p = 64 if c == 0 else 128
                nc.scalar.activation(sil[0:p, c % 2, :], GU[c % 2][0:p, 0:N], ACT.Silu).then_inc(s_sil, 1)

            act.wait_ge(s_bias, 32)
            act.wait_ge(s_zero, 1)
            t_split(0)
            qk_bias(0)
            exps(0)
            pt_copy(0)
            gate(0)
            ht_split(0)
            with act.Fori(1, NG) as g:
                silu(g - 1, 0)
                t_split(g)
                qk_bias(g)
                silu(g - 1, 1)
                exps(g)
                silu(g - 1, 2)
                silu(g - 1, 3)
                pt_copy(g)
                silu(g - 1, 4)
                gate(g)
                for c in range(5, NF):
                    silu(g - 1, c)
                ht_split(g)
            for c in range(NF):
                silu(NG - 1, c)

        @block.vector
        def _(dve):
            def alone(s, value):
                dve.wait_ge(s, value)
                dve.sem_inc(s_waited, 1)

            def ln1_stats(g):
                for b in range(GB):
                    nc.vector.bn_stats(st1[:, b, :], x_all[:, g * GB + b, :]).then_inc(s_st1, 1)
                alone(s_st1, GB * (g + 1))
                for b in range(GB):
                    nc.vector.bn_aggr(mv1[:, b, :], st1[:, b, :]).then_inc(s_mv1, 1)

            def ln1_apply(g):
                dve.wait_ge(s_rs1, g + 1)
                for b in range(GB):
                    nc.vector.tensor_scalar(xn[:, b, :], x_all[:, g * GB + b, :], mv1[:, b, 0:1], rs1[:, b:b + 1],
                                            ALU.subtract, ALU.mult).then_inc(s_xn, 1)

            def t_rest(g):
                dve.wait_ge(s_thi, g + 1)
                nc.vector.tensor_tensor(t_lo[:].rearrange("p s n -> p (s n)"), BT[:],
                                        t_hi[:].rearrange("p s n -> p (s n)").bitcast(fp32),
                                        ALU.subtract).then_inc(s_tlo, 1)

            def qk_bias(g):
                dve.wait_ge(s_qk, 2 * g + 2)
                for n in (KS, QS):
                    nc.vector.tensor_scalar(qk[:, n, :], BK[:, (n - 2) * N:(n - 1) * N], bcol[:, n:n + 1], None,
                                            ALU.add).then_inc(s_qkd, 1)

            def row_max(g):
                dve.wait_ge(s_s, g + 1)
                sc = BQ[:].rearrange("p (b s k) -> p b s k", b=GB, s=2)
                for side, k in ((0, C), (1, 128)):
                    nc.vector.tensor_reduce(mx[:, :, side], sc[:, :, side, 0:k], AX, ALU.max).then_inc(s_mx, 1)
                dve.wait_ge(s_mx, 2 * (g + 1))
                nc.vector.tensor_scalar(nmx[:], mx[:], -SCALE, None, ALU.mult).then_inc(s_nmx, 1)

            def values(g, b):
                dve.wait_ge(s_v, GB * g + b + 1)
                nc.vector.tensor_tensor(val[:, b, :, :].rearrange("p s n -> p (s n)"), VB[b][:],
                                        vbias[:].rearrange("p s n -> p (s n)"), ALU.add).then_inc(s_ve, 1)

            def normalise(g):
                dve.wait_ge(s_e, 4 * (g + 1))
                nc.vector.reciprocal(rinv[:], rsum[:]).then_inc(s_ri, 1)
                dve.wait_ge(s_ri, g + 1)
                nc.vector.tensor_tensor(probn[:].rearrange("p b s k -> p (b s) k"),
                                        prob[:].rearrange("p b s k -> p (b s) k"),
                                        rinv[:].rearrange("p b s -> p (b s)").unsqueeze(2).broadcast_to([128, 2 * GB, 128]),
                                        ALU.mult).then_inc(s_pn, 1)

            def mix(g, b):
                dve.wait_ge(s_g, GB * g + b + 1)
                nc.vector.scalar_tensor_tensor(mixd[:, b, :], gt[:, b, :], 1.0, VB[b][:, 0:128],
                                               ALU.add, ALU.mult).then_inc(s_md, 1)
                nc.vector.scalar_tensor_tensor(xc[:, b, :], VB[b][:, 256:384], -2.0, x_all[:, g * GB + b, :],
                                               ALU.mult, ALU.add).then_inc(s_xc, 1)

            def ln2_stats(g):
                dve.wait_ge(s_x2, g + 1)
                for b in range(GB):
                    nc.vector.bn_stats(st2[:, b, :], x2[:, b, :]).then_inc(s_st2, 1)
                alone(s_st2, GB * (g + 1))
                for b in range(GB):
                    nc.vector.bn_aggr(mv2[:, b, :], st2[:, b, :]).then_inc(s_mv2, 1)

            def ln2_apply(g):
                dve.wait_ge(s_rs2, g + 1)
                if not (isinstance(g, int) and g == 0):
                    dve.wait_ge(s_x2h, g)
                for b in range(GB):
                    nc.vector.tensor_scalar(h[:, b, :], x2[:, b, :], mv2[:, b, 0:1], rs2[:, b:b + 1],
                                            ALU.subtract, ALU.mult).then_inc(s_h, 1)

            def ht_rest(g):
                dve.wait_ge(s_hthi, g + 1)
                nc.vector.tensor_tensor(hT_lo[:], BQ[:, 0:N], hT_hi[:].bitcast(fp32),
                                        ALU.subtract).then_inc(s_htlo, 1)

            def router_a(g):
                dve.wait_ge(s_rl, g + 1)
                nc.vector.tensor_tensor(lg[:], BK[:, 0:GB * E].rearrange("p (b e) -> p b e", b=GB),
                                        brow[:, 384:384 + E].unsqueeze(1).broadcast_to([128, GB, E]), ALU.add).then_inc(s_lg, 1)
                alone(s_lg, g + 1)
                for b in range(GB):
                    nc.vector.max(top[:, b, :], lg[:, b, :]).then_inc(s_top, 1)
                alone(s_top, GB * (g + 1))
                for b in range(GB):
                    nc.vector.max_index(topi[:, b, :], top[:, b, :], lg[:, b, :]).then_inc(s_topi, 1)

            def router_b(g):
                dve.wait_ge(s_topi, GB * (g + 1))
                nc.vector.tensor_tensor(oh[:],
                                        iota.unsqueeze(1).unsqueeze(1).broadcast_to([128, GB, 2, E]),
                                        topi[:, :, 0:2].unsqueeze(3).broadcast_to([128, GB, 2, E]),
                                        ALU.is_equal).then_inc(s_oh, 1)
                dve.wait_ge(s_ez1, g + 1)
                nc.vector.reciprocal(sg[:], ez1[:]).then_inc(s_sg, 1)
                dve.wait_ge(s_sg, g + 1)
                nc.vector.tensor_tensor(sgs[:], sg[:, :, 0], sg[:, :, 1], ALU.add).then_inc(s_sgs, 1)
                dve.wait_ge(s_sgs, g + 1)
                nc.vector.reciprocal(sgr[:], sgs[:]).then_inc(s_sgr, 1)
                dve.wait_ge(s_sgr, g + 1)
                nc.vector.tensor_tensor(wt[:], sg[:], sgr[:].unsqueeze(2).broadcast_to([128, GB, 2]), ALU.mult).then_inc(s_wt, 1)
                dve.wait_ge(s_oh, g + 1)
                dve.wait_ge(s_wt, g + 1)
                nc.vector.tensor_tensor(ohw[:], oh[:], wt[:].unsqueeze(3).broadcast_to([128, GB, 2, E]), ALU.mult).then_inc(s_ohw, 1)
                dve.wait_ge(s_ohw, g + 1)
                nc.vector.tensor_tensor(wsum[:], ohw[:, :, 0, :], ohw[:, :, 1, :], ALU.add).then_inc(s_ws, 1)
                dve.wait_ge(s_ws, g + 1)
                nc.vector.tensor_copy(wst_r[:, :, 0:E], wsum[:]).then_inc(s_whi, 1)
                dve.wait_ge(s_whi, g + 1)
                nc.vector.tensor_tensor(wst_r[:, :, E:2 * E], wsum[:], wst[:, :, 0:E], ALU.subtract).then_inc(s_wlo, 1)

            def weights_copy(g):
                dve.wait_ge(s_wtt, g + 1)
                nc.vector.tensor_copy(wT[:], BV[:, 0:N]).then_inc(s_wT, 1)

            def up_mul(g, c):
                dve.wait_ge(s_sil, NF * g + c + 1)
                if c == 0:
                    nc.vector.tensor_tensor(hid0[0:64, :], GU[0][64:128, 0:N], sil[0:64, 0, :], ALU.mult)\
                      .then_inc(s_mul, 1)
                else:
                    nc.vector.tensor_tensor(mul[:, c % 2, :], GU[c % 2][:, N:2 * N], sil[:, c % 2, :], ALU.mult)\
                      .then_inc(s_mul, 1)

            def weigh(g, c):
                dve.wait_ge(s_mul, NF * g + c + 1)
                dve.wait_ge(s_wb, CH * g + c)
                if c >= 3:
                    dve.wait_ge(s_d, NF * g + c - 1)
                nc.vector.tensor_tensor(hid[:, c % 2, :], WB[:, 0:N], mul[:, c % 2, :], ALU.mult).then_inc(s_hid, 1)

            def ffn(g, c):
                up_mul(g, c)
                if c:
                    weigh(g, c)

            def finish(g):
                dve.wait_ge(s_d, NF * (g + 1))
                dve.wait_ge(s_x2h, g + 1)
                dve.wait_ge(s_out, 16 * (g + 1))
                nc.vector.tensor_tensor(yout[:].rearrange("p b d -> p (b d)"), Y[:, 0:N],
                                        x2h[:].rearrange("p b d -> p (b d)"), ALU.add).then_inc(s_y, 1)

            dve.sem_inc(s_y, 1)
            nc.vector.memset(ctx_t[96:128, :, :], 0.0).then_inc(s_pad, 1)
            nc.vector.memset(wd[64:128, 0, :], 0.0).then_inc(s_pad, 1)
            dve.wait_ge(s_xin[0], 16)
            ln1_stats(0)
            dve.wait_ge(s_aw, 16)
            nc.vector.tensor_copy(wqk_hi[:], aw[:, 0:4, :]).then_inc(s_qkw, 1)
            ln1_apply(0)
            dve.wait_ge(s_qkw, 1)
            nc.vector.tensor_tensor(wqk_lo[:], aw[:, 0:4, :], wqk_hi[:].bitcast(fp32), ALU.subtract).then_inc(s_qkw, 1)
            nc.vector.tensor_scalar(wv[:, 0, 0:128], aw[:, 4, :], -0.5, None, ALU.mult).then_inc(s_wv, 1)
            nc.vector.tensor_scalar(wv[:, 1, 0:128], aw[:, 5, :], 0.5, None, ALU.mult).then_inc(s_wv, 1)
            t_rest(0)
            dve.wait_ge(s_prod, 1)
            nc.vector.tensor_copy(wv[:, 0, 128:256], GU[0][:, 0:128]).then_inc(s_wv, 1)
            nc.vector.tensor_copy(wv[:, 1, 128:256], GU[0][:, 128:256]).then_inc(s_wv, 1)
            dve.wait_ge(s_wv, 4)
            nc.vector.tensor_copy(wv_hi[:], wv[:]).then_inc(s_wvs, 1)
            dve.wait_ge(s_wvs, 1)
            nc.vector.tensor_tensor(wv_lo[:], wv[:], wv_hi[:].bitcast(fp32), ALU.subtract).then_inc(s_wvs, 1)
            qk_bias(0)
            dve.wait_ge(s_bias, 32)
            nc.vector.tensor_scalar(vbias[:, 0, 0:128], brow[:, 0:128], -0.5, None, ALU.mult).then_inc(s_vb, 1)
            nc.vector.tensor_scalar(vbias[:, 1, 0:128], brow[:, 128:256], 0.5, None, ALU.mult).then_inc(s_vb, 1)
            nc.vector.tensor_tensor(vbias[:, 0, 128:256], GU[0][:, 256:384], brow[:, 256:384], ALU.add).then_inc(s_vb, 1)
            nc.vector.tensor_copy(vbias[:, 1, 128:256], GU[0][:, 384:512]).then_inc(s_vb, 1)
            row_max(0)
            dve.wait_ge(s_vb, 4)
            values(0, 0)
            values(0, 1)
            dve.wait_ge(s_zero, 1)
            normalise(0)
            dve.wait_ge(s_xin[1], 16)
            ln1_stats(1)
            ln1_apply(1)
            mix(0, 0)
            mix(0, 1)
            ln2_stats(0)
            ln2_apply(0)
            ht_rest(0)
            router_a(0)
            with dve.Fori(1, NG - 1) as g:
                t_rest(g)
                router_b(g - 1)
                ffn(g - 1, 0)
                qk_bias(g)
                weights_copy(g - 1)
                row_max(g)
                ffn(g - 1, 1)
                values(g, 0)
                values(g, 1)
                normalise(g)
                ln1_stats(g + 1)
                ffn(g - 1, 2)
                ln1_apply(g + 1)
                ffn(g - 1, 3)
                ffn(g - 1, 4)
                mix(g, 0)
                mix(g, 1)
                ffn(g - 1, 5)
                ln2_stats(g)
                ffn(g - 1, 6)
                ln2_apply(g)
                ffn(g - 1, 7)
                ffn(g - 1, 8)
                ht_rest(g)
                router_a(g)
                finish(g - 1)
            g = NG - 1
            t_rest(g)
            router_b(g - 1)
            ffn(g - 1, 0)
            qk_bias(g)
            weights_copy(g - 1)
            row_max(g)
            ffn(g - 1, 1)
            values(g, 0)
            values(g, 1)
            normalise(g)
            ffn(g - 1, 2)
            ffn(g - 1, 3)
            ffn(g - 1, 4)
            mix(g, 0)
            mix(g, 1)
            ffn(g - 1, 5)
            ln2_stats(g)
            ffn(g - 1, 6)
            ln2_apply(g)
            ffn(g - 1, 7)
            ffn(g - 1, 8)
            ht_rest(g)
            router_a(g)
            finish(g - 1)
            router_b(g)
            ffn(g, 0)
            weights_copy(g)
            for c in range(1, NF):
                ffn(g, c)
            finish(g)

        @block.tensor
        def _(pe):
            mm = nc.tensor.matmul

            def split3(dst, w_hi, w_lo, r_hi, r_lo):
                mm(dst, w_hi, r_hi, start=True, stop=False)
                mm(dst, w_hi, r_lo, start=False, stop=False)
                return mm(dst, w_lo, r_hi, start=False, stop=True)

            def transpose_in(g):
                pe.wait_ge(s_xn, GB * (g + 1))
                pe.wait_ge(s_ctx, 16 * (g + 1))
                for b in range(GB):
                    nc.tensor.transpose(BT[:, b * 128:(b + 1) * 128], xn[:, b, :], ident)
                for b in range(GB):
                    last = nc.tensor.transpose(BT[:, N + b * 128:N + (b + 1) * 128], ctx_t[:, b, :], ident)
                last.then_inc(s_t, 1)

            def project(g):
                pe.wait_ge(s_thi, g + 1)
                pe.wait_ge(s_tlo, g + 1)
                for n in range(4):
                    side, dst = n // 2, (BQ, BK)[n // 2][:, (n % 2) * N:(n % 2 + 1) * N]
                    last = split3(dst, wqk_hi[:, n, :], wqk_lo[:, n, :], t_hi[:, side, :], t_lo[:, side, :])
                    if n % 2:
                        last.then_inc(s_qk, 1)

            def scores(g):
                pe.wait_ge(s_qka, 2 * (g + 1))
                pe.wait_ge(s_qkd, 2 * (g + 1))
                for b in range(GB):
                    at = slice(b * 128, (b + 1) * 128)
                    mm(BQ[:, b * 256:b * 256 + C], qk[:, QC, at], qk[:, KS, b * 128:b * 128 + C], start=True, stop=True)
                    last = mm(BQ[:, b * 256 + 128:b * 256 + 256], qk[:, QS, at], qk[:, KC, at], start=True, stop=True)
                last.then_inc(s_s, 1)

            def values(g, b):
                for side in range(2):
                    at = slice(b * 128, (b + 1) * 128)
                    last = split3(VB[b][:, side * 256:(side + 1) * 256], t_hi[:, 1 - side, at], t_lo[:, 1 - side, at],
                                  wv_hi[:, side, :], wv_lo[:, side, :])
                last.then_inc(s_v, 1)

            def probs_t(g):
                pe.wait_ge(s_pn, g + 1)
                for b in range(GB):
                    nc.tensor.transpose(BK[:, b * 256:b * 256 + 128], probn[:, b, 0, :], ident)
                    last = mm(BK[:, b * 256 + 128:b * 256 + 256], probn[0:C, b, 1, :], interpT[0:C, :],
                              start=True, stop=True)
                last.then_inc(s_pt, 1)

            def mix(g, b):
                if b == 0:
                    pe.wait_ge(s_pte, g + 1)
                pe.wait_ge(s_ve, GB * g + b + 1)
                mm(VB[b][:, 0:256], pT[0:C, b, 0, :], val[0:C, b, 0, :], start=True, stop=False)
                mm(VB[b][:, 0:256], pT[:, b, 1, :], val[:, b, 1, :], start=False, stop=True)
                mm(VB[b][:, 256:384], pT[0:C, b, 0, :], val[0:C, b, 0, 0:128], start=True, stop=True)\
                  .then_inc(s_av, 1)

            def transpose_h(g):
                pe.wait_ge(s_h, GB * (g + 1))
                for b in range(GB):
                    last = nc.tensor.transpose(BQ[:, b * 128:(b + 1) * 128], h[:, b, :], ident)
                last.then_inc(s_ht, 1)

            def logits(g):
                pe.wait_ge(s_hthi, g + 1)
                pe.wait_ge(s_htlo, g + 1)
                for b in range(GB):
                    at = slice(b * 128, (b + 1) * 128)
                    mm(BK[:, b * E:(b + 1) * E], hT_hi[:, at].bitcast(fp32), gate_w[:], start=True, stop=False)
                    last = mm(BK[:, b * E:(b + 1) * E], hT_lo[:, at].bitcast(fp32), gate_w[:], start=False, stop=True)
                last.then_inc(s_rl, 1)

            def weights_t(g):
                pe.wait_ge(s_wlo, g + 1)
                for b in range(GB):
                    last = nc.tensor.transpose(BV[:, b * 128:(b + 1) * 128], wst[:, b, :], ident)
                last.then_inc(s_wtt, 1)

            def gate_up(g, c):
                if c >= 2:
                    pe.wait_ge(s_mul, NF * g + c - 1)
                if c == 0:
                    split3(GU[0][:, 0:N], wsh_hi[:], wsh_lo[:], hT_hi[:], hT_lo[:]).then_inc(s_gu, 1)
                    return
                at = slice((c - 1) * 128, c * 128)
                split3(GU[c % 2][:, 0:N], wg_hi[:, at], wg_lo[:, at], hT_hi[:], hT_lo[:])
                split3(GU[c % 2][:, N:2 * N], wu_hi[:, at], wu_lo[:, at], hT_hi[:], hT_lo[:]).then_inc(s_gu, 1)

            def spread(g, c):
                if c == 1:
                    pe.wait_ge(s_wT, g + 1)
                else:
                    pe.wait_ge(s_hid, CH * g + c - 1)
                mm(WB[:, 0:N], sel[:, c - 1, :], wT[:], start=True, stop=True).then_inc(s_wb, 1)

            def down(g, c):
                if c == 0:
                    pe.wait_ge(s_mul, NF * g + 1)
                    pe.wait_ge(s_y, g + 1)
                else:
                    pe.wait_ge(s_hid, CH * g + c)
                src = hid0[:] if c == 0 else hid[:, c % 2, :]
                for b in range(GB):
                    last = mm(Y[:, b * 128:(b + 1) * 128], src[:, b * 128:(b + 1) * 128], wd[:, c, :],
                              start=(c == 0 and b == 0), stop=(c == NF - 1), skip_group_check=True)
                last.then_inc(s_d, 1)

            pe.wait_ge(s_cst, 16)
            pe.wait_ge(s_pad, 2)
            transpose_in(0)
            pe.wait_ge(s_aw, 16)
            pe.wait_ge(s_bias, 32)
            for side in range(2):
                mm(GU[0][:, side * 128:(side + 1) * 128], aw[:, 6 + side, :], aw[:, 8 + side, :], start=True, stop=True)
            for side in range(2):
                last = mm(GU[0][:, 256 + side * 128:384 + side * 128], bcol[:, 4 + side:5 + side].broadcast_to([128, 128]),
                          aw[:, 8 + side, :], start=True, stop=True)
            last.then_inc(s_prod, 1)
            pe.wait_ge(s_qkw, 2)
            project(0)
            scores(0)
            pe.wait_ge(s_wvs, 2)
            values(0, 0)
            values(0, 1)
            probs_t(0)
            mix(0, 0)
            mix(0, 1)
            transpose_h(0)
            pe.wait_ge(s_ffn, 16 * 6)
            logits(0)
            pe.wait_ge(s_fw, 7)
            pe.wait_ge(s_vb, 4)
            with pe.Fori(1, NG) as g:
                f = g - 1
                transpose_in(g)
                gate_up(f, 0)
                project(g)
                gate_up(f, 1)
                weights_t(f)
                down(f, 0)
                scores(g)
                spread(f, 1)
                gate_up(f, 2)
                values(g, 0)
                down(f, 1)
                values(g, 1)
                gate_up(f, 3)
                spread(f, 2)
                probs_t(g)
                down(f, 2)
                gate_up(f, 4)
                spread(f, 3)
                mix(g, 0)
                down(f, 3)
                mix(g, 1)
                for c in range(5, NF):
                    gate_up(f, c)
                    spread(f, c - 1)
                    down(f, c - 1)
                transpose_h(g)
                spread(f, NF - 1)
                logits(g)
                down(f, NF - 1)
            f = NG - 1
            gate_up(f, 0)
            gate_up(f, 1)
            weights_t(f)
            down(f, 0)
            spread(f, 1)
            for c in range(2, NF):
                gate_up(f, c)
                down(f, c - 1)
                spread(f, c)
            down(f, NF - 1)


def kernel(x, ctx_1024, L0_xattn_Wq_c, L0_xattn_bq_c, L0_xattn_Wk_s, L0_xattn_bk_s, L0_xattn_Wv_s, L0_xattn_bv_s,
           L0_xattn_Wq_s, L0_xattn_bq_s, L0_xattn_Wk_c, L0_xattn_bk_c, L0_xattn_Wv_c, L0_xattn_bv_c, L0_xattn_Wg,
           L0_xattn_bg, L0_ffn_gate_w, L0_ffn_gate_b, L0_ffn_shared_wg, L0_ffn_shared_wu, L0_ffn_shared_wd,
           L0_ffn_experts_wg, L0_ffn_experts_wu, L0_ffn_experts_wd):
    import numpy as np
    import concourse.bacc as bacc
    from concourse.bass_utils import run_bass_kernel_spmd

    def arr(a):
        return np.ascontiguousarray(a)

    x, ctx_1024 = arr(x), arr(ctx_1024)
    D, C = x.shape[2], ctx_1024.shape[1]
    T = x.shape[1]
    E = L0_ffn_gate_w.shape[1]
    H = L0_ffn_shared_wg.shape[1]
    wg_gate = arr(L0_xattn_Wg)
    attn_w = arr(np.concatenate([arr(L0_xattn_Wq_c).T, arr(L0_xattn_Wk_c).T, arr(L0_xattn_Wk_s).T, arr(L0_xattn_Wq_s).T,
                                 arr(L0_xattn_Wv_s).T, arr(L0_xattn_Wv_c).T, arr(L0_xattn_Wv_s), arr(L0_xattn_Wv_c),
                                 wg_gate[:, :D].T, wg_gate[:, D:].T], axis=1))
    bias_col = arr(np.stack([arr(b) for b in (L0_xattn_bq_c, L0_xattn_bk_c, L0_xattn_bk_s, L0_xattn_bq_s,
                                              L0_xattn_bv_s, L0_xattn_bv_c)], axis=1))
    bias_row = arr(np.concatenate([arr(L0_xattn_bv_s), arr(L0_xattn_bv_c), arr(L0_xattn_bg), arr(L0_ffn_gate_b)]))
    wg = arr(np.transpose(arr(L0_ffn_experts_wg), (1, 0, 2)).reshape(D, E * H))
    wu = arr(np.transpose(arr(L0_ffn_experts_wu), (1, 0, 2)).reshape(D, E * H))
    wsh = arr(np.concatenate([arr(L0_ffn_shared_wg), arr(L0_ffn_shared_wu), arr(L0_ffn_gate_w)], axis=1))
    wd = arr(np.concatenate([arr(L0_ffn_shared_wd), arr(L0_ffn_experts_wd).reshape(E * H, D)], axis=0))

    consts = np.zeros((128, 256 + (E * H // 128) * 128 + E), np.float32)
    consts[:, 0:128] = np.eye(128, dtype=np.float32)
    pos = np.clip((np.arange(T, dtype=np.float32) + np.float32(0.5)) * np.float32(C / T) - np.float32(0.5), 0, C - 1)
    lo = np.floor(pos).astype(np.int32)
    for t in range(T):
        w = pos[t] - np.float32(lo[t])
        consts[lo[t], 128 + t] += 1 - w
        consts[min(lo[t] + 1, C - 1), 128 + t] += w
    for c in range(E * H // 128):
        for m in range(128):
            e = (128 * c + m) // H
            consts[e, 256 + 128 * c + m] = 1
            consts[E + e, 256 + 128 * c + m] = 1
    consts[:, -E:] = np.arange(E, dtype=np.float32)

    arrays = dict(x=x, ctx_in=ctx_1024, attn_w=attn_w, bias_col=bias_col, bias_row=bias_row, const_in=consts,
                  wg_in=wg, wu_in=wu, wsh_in=wsh, wd_in=wd)
    nc = bacc.Bacc("TRN2", target_bir_lowering=False, num_devices=1)
    args = [nc.dram_tensor(name, a.shape, mybir.dt.from_np(a.dtype), kind="ExternalInput").ap()
            for name, a in arrays.items()]
    out = nc.dram_tensor("out", x.shape, mybir.dt.float32, kind="ExternalOutput").ap()
    xattn_ffn_kernel(nc, *args, out)
    return run_bass_kernel_spmd(nc, [arrays], core_ids=[0]).results[0]["out"]
```

```python
import concourse.bass as bass
from concourse import mybir
from contextlib import ExitStack




def xattn_ffn_kernel(nc, x, ctx_in, attn_w, bias_col, bias_row, const_in, wg_in, wu_in, wsh_in, wd_in, out):
    fp32, f32r, u32 = mybir.dt.float32, mybir.dt.float32r, mybir.dt.uint32
    ALU = mybir.AluOpType
    ACT = mybir.ActivationFunctionType
    AX = mybir.AxisListType.X

    B, T, D = x.shape
    C = ctx_in.shape[1]
    GB = 2
    NG = B // GB
    N = GB * T
    E = 16
    H = 64
    CH = E * H // 128
    NF = CH + 1
    RING = 4
    SCALE = float(D) ** -0.5
    EPS = 1e-5
    QC, KC, KS, QS = range(4)

    ctx = ExitStack()
    with ctx:
        def sb(name, shape, dt=fp32):
            return ctx.enter_context(nc.sbuf_tensor(name, shape, dt))

        def pb(name):
            return ctx.enter_context(nc.psum_tensor(name, [128, 512], fp32))

        def sem(name):
            return ctx.enter_context(nc.semaphore(name))

        aw = sb("aw", [128, 10, 128])
        bcol = sb("bcol", [128, 6])
        brow = sb("brow", [128, 3 * 128 + E])
        cst = sb("cst", [128, 2 * 128 + CH * 128 + E])
        ident = cst[:, 0:128]
        interpT = cst[:, 128:256]
        sel_f = cst[:, 256:256 + CH * 128]
        iota = cst[:, 256 + CH * 128:]
        wqk_hi = sb("wqk_hi", [128, 4, 128], f32r)
        wqk_lo = sb("wqk_lo", [128, 4, 128], f32r)
        wv = sb("wv", [128, 2, 256])
        wv_hi = sb("wv_hi", [128, 2, 256], f32r)
        wv_lo = sb("wv_lo", [128, 2, 256], f32r)
        vbias = sb("vbias", [128, 2, 256])
        wg = sb("wg", [128, E * H])
        wu = sb("wu", [128, E * H])
        wsh = sb("wsh", [128, 128])
        wg_hi = sb("wg_hi", [128, E * H], f32r)
        wg_lo = sb("wg_lo", [128, E * H], f32r)
        wu_hi = sb("wu_hi", [128, E * H], f32r)
        wu_lo = sb("wu_lo", [128, E * H], f32r)
        wsh_hi = sb("wsh_hi", [128, 128], f32r)
        wsh_lo = sb("wsh_lo", [128, 128], f32r)
        wd = sb("wd", [128, NF, 128])
        gate_w = sb("gate_w", [128, E])
        sel = sb("sel", [128, CH, 128], f32r)
        powc = sb("powc", [128, GB, 2])
        negc = sb("negc", [128, GB, 2])
        onec = sb("onec", [128, GB, 2])
        epsc = sb("epsc", [128, B])
        halfc = sb("halfc", [128, B])

        x_all = sb("x_all", [128, B, 128])
        ctx_t = sb("ctx_t", [128, GB, 128])
        st1 = sb("st1", [128, B, 6])
        mv1 = sb("mv1", [128, B, 2])
        ve1 = sb("ve1", [128, B])
        rs1 = sb("rs1", [128, B])
        xn = sb("xn", [128, GB, 128])
        t_hi = sb("t_hi", [128, 2, N], f32r)
        t_lo = sb("t_lo", [128, 2, N], f32r)
        qk = sb("qk", [128, 4, N])
        val = sb("val", [128, GB, 2, 256])
        mx = sb("mx", [128, GB, 2])
        nmx = sb("nmx", [128, GB, 2])
        prob = sb("prob", [128, GB, 2, 128])
        rsum = sb("rsum", [128, GB, 2])
        rinv = sb("rinv", [128, GB, 2])
        probn = sb("probn", [128, GB, 2, 128])
        pT = sb("pT", [128, GB, 2, 128])
        gt = sb("gt", [128, GB, 128])
        mixd = sb("mixd", [128, GB, 128])
        xc = sb("xc", [128, GB, 128])
        x2 = sb("x2", [128, GB, 128])
        st2 = sb("st2", [128, GB, 6])
        mv2 = sb("mv2", [128, GB, 2])
        ve2 = sb("ve2", [128, GB])
        rs2 = sb("rs2", [128, GB])
        h = sb("h", [128, GB, 128])
        x2h = sb("x2h", [128, GB, 128])
        hT = sb("hT", [128, N])
        hT_hi = sb("hT_hi", [128, N], f32r)
        hT_lo = sb("hT_lo", [128, N], f32r)
        lg = sb("lg", [128, GB, E])
        top = sb("top", [128, GB, 8])
        topi = sb("topi", [128, GB, 8], u32)
        nz = sb("nz", [128, GB, 2])
        ez = sb("ez", [128, GB, 2])
        ez1 = sb("ez1", [128, GB, 2])
        sg = sb("sg", [128, GB, 2])
        sgs = sb("sgs", [128, GB])
        sgr = sb("sgr", [128, GB])
        wt = sb("wt", [128, GB, 2])
        oh = sb("oh", [128, GB, 2, E])
        ohw = sb("ohw", [128, GB, 2, E])
        wsum = sb("wsum", [128, GB, E])
        wst = sb("wst", [128, GB, 128])
        wst_r = wst[:].bitcast(f32r)
        wT = sb("wT", [128, N], f32r)
        sil = sb("sil", [128, 2, N])
        mul = sb("mul", [128, RING, N])
        wbs = sb("wbs", [128, CH, N])
        hid = sb("hid", [128, RING, N])
        hid0 = sb("hid0", [128, N])
        yout = sb("yout", [128, GB, 128])
        warm = sb("warm", [128, 2])

        GU = [pb("GU0"), pb("GU1")]
        WB = pb("WB")
        Y = pb("Y")
        BQ = pb("BQ")
        BK = pb("BK")
        BT = pb("BT")
        BV = pb("BV")
        VALB = [BK, BT]
        MIXB = [BT, BV]

        s_cst, s_cst2, s_bias, s_ctx, s_out = (sem(n) for n in
            ("identity_in", "selection_in", "bias_in", "ctx_in_sem", "out_stored"))
        s_aw = [sem("qk_w_in"), sem("value_w_in")]
        s_ffn = [sem(n) for n in ("gate_w_in", "up_w_in", "shared_w_in", "router_down_w_in")]
        s_small = sem("small_consts_set")
        s_hi, s_lo, s_sel = sem("ffn_hi_parts"), sem("ffn_lo_parts"), sem("selection_ready")
        s_xin = [sem(f"x_in_{i}") for i in range(2)]
        s_zero = sem("zeros_set")
        s_pad = sem("row_padding_set")
        s_qkw = sem("qk_weights_split")
        s_prod = sem("value_gate_products")
        s_wv = sem("value_weights_built")
        s_wvs = sem("value_weights_split")
        s_vb = sem("value_bias_built")
        s_st1, s_mv1, s_ve1, s_rs1, s_xn = (sem(n) for n in ("stats1", "meanvar1", "vareps1", "rstd1", "xn_ready"))
        s_t, s_thi, s_tlo = sem("transposed"), sem("t_hi_ready"), sem("t_lo_ready")
        s_qk, s_qka, s_qkd = sem("qk_projected"), sem("qk_x_ready"), sem("qk_ctx_ready")
        s_s, s_mx, s_nmx, s_e, s_ri, s_pn = (sem(n) for n in
            ("scores_done", "row_max", "neg_max", "exp_done", "inv_sum", "probs_normed"))
        s_v, s_ve = sem("values_projected"), sem("values_ready")
        s_pt, s_pte = sem("probs_transposed"), sem("pT_ready")
        s_av, s_g, s_md, s_xc, s_x2 = (sem(n) for n in
            ("mix_products", "gate_tanh", "mix_diff", "mix_base", "x2_ready"))
        s_st2, s_mv2, s_ve2, s_rs2, s_h, s_x2h = (sem(n) for n in
            ("stats2", "meanvar2", "vareps2", "rstd2", "h_ready", "x2h_ready"))
        s_hT = sem("hT_ready")
        s_ht, s_hthi, s_htlo = sem("h_transposed"), sem("hT_hi_ready"), sem("hT_lo_ready")
        s_rl, s_lg, s_top, s_topi, s_nz, s_ez, s_ez1 = (sem(n) for n in
            ("router_logits", "logits_biased", "top8", "top8_index", "neg_logit", "exp_neg_logit", "one_plus_exp"))
        s_sg, s_sgs, s_sgr, s_wt, s_oh, s_ohw, s_ws, s_whi, s_wlo = (sem(n) for n in
            ("sigmoid", "sigmoid_sum", "sigmoid_inv", "top2_weights", "one_hot", "one_hot_weighted",
             "weights_row", "weights_hi", "weights_lo"))
        s_wtt, s_wT = sem("weights_transposed"), sem("wT_ready")
        s_gu, s_sil, s_mul, s_wb, s_wbs, s_hid, s_hidl, s_d = (sem(n) for n in
            ("gate_up_done", "silu_done", "mul_done", "weights_spread", "weights_on_rows", "hidden_ready", "last_hidden_ready", "down_done"))
        s_y = sem("y_ready")
        s_waited = sem("waits_alone")

        block = ctx.enter_context(nc.Block())


        @block.sync
        def _(sp):
            sp.sem_inc(s_out, 16)
            sp.dma_start(x_all[:, 0:GB, :], x[0:GB].rearrange("b p d -> p b d")).then_inc(s_xin[0], 16)
            sp.wait_ge(s_pad, 1)
            sp.dma_start(ctx_t[0:C, :, :], ctx_in[0:GB].rearrange("b p d -> p b d")).then_inc(s_ctx, 16)
            sp.dma_start(aw[:, 0:4, :], attn_w[:, 0:512].rearrange("p (n d) -> p n d", n=4)).then_inc(s_aw[0], 16)
            sp.dma_start(aw[:, 4:10, :], attn_w[:, 512:1280].rearrange("p (n d) -> p n d", n=6)).then_inc(s_aw[1], 16)
            sp.dma_start(x_all[:, GB:B, :], x[GB:B].rearrange("b p d -> p b d")).then_inc(s_xin[1], 16)
            sp.dma_start(wg[:], wg_in).then_inc(s_ffn[0], 16)
            sp.dma_start(wu[:], wu_in).then_inc(s_ffn[1], 16)

            def load_ctx(g):
                sp.wait_ge(s_t, g)
                sp.dma_start(ctx_t[0:C, :, :],
                             ctx_in[bass.ds(g * GB, GB)].rearrange("b p d -> p b d")).then_inc(s_ctx, 16)

            def store(g):
                sp.wait_ge(s_y, g + 2)
                sp.dma_start(out[bass.ds(g * GB, GB)].rearrange("b p d -> p b d"), yout[:]).then_inc(s_out, 16)

            load_ctx(1)
            load_ctx(2)
            with sp.Fori(1, NG - 2) as g:
                load_ctx(g + 2)
                store(g - 1)
            for g in range(NG - 3, NG):
                store(g)
            sp.wait_ge(s_out, 16 * (NG + 1))

        @block.gpsimd
        def _(pool):
            nc.gpsimd.memset(halfc[:], -0.5)
            nc.gpsimd.memset(powc[:], 2.718281828459045)
            nc.gpsimd.memset(negc[:], -1.0)
            nc.gpsimd.memset(onec[:], 1.0)
            nc.gpsimd.memset(epsc[:], EPS).then_inc(s_small, 1)
            nc.gpsimd.memset(prob[:], 0.0)
            nc.gpsimd.memset(wst[:], 0.0)
            nc.gpsimd.memset(hid0[:], 0.0).then_inc(s_zero, 1)

            def ln1(b0, b1, n):
                pool.wait_ge(s_mv1, b1)
                nc.gpsimd.tensor_tensor(ve1[:, b0:b1], mv1[:, b0:b1, 1], epsc[:, b0:b1], ALU.add).then_inc(s_ve1, 1)
                pool.wait_ge(s_ve1, n)
                nc.gpsimd.tensor_tensor(rs1[:, b0:b1], ve1[:, b0:b1], halfc[:, b0:b1], ALU.pow).then_inc(s_rs1, 1)

            def ln2(g):
                pool.wait_ge(s_mv2, GB * (g + 1))
                nc.gpsimd.tensor_tensor(ve2[:], mv2[:, :, 1], epsc[:, 0:GB], ALU.add).then_inc(s_ve2, 1)
                pool.wait_ge(s_ve2, g + 1)
                nc.gpsimd.tensor_tensor(rs2[:], ve2[:], halfc[:, 0:GB], ALU.pow).then_inc(s_rs2, 1)

            def mix(g):
                pool.wait_ge(s_md, GB * (g + 1))
                pool.wait_ge(s_xc, GB * (g + 1))
                if not (isinstance(g, int) and g == 0):
                    pool.wait_ge(s_x2h, g)
                nc.gpsimd.tensor_tensor(x2[:], mixd[:], xc[:], ALU.add).then_inc(s_x2, 1)

            def residual(g):
                pool.wait_ge(s_y, g + 1)
                pool.wait_ge(s_h, GB * (g + 1))
                nc.gpsimd.tensor_tensor(x2h[:], x2[:], h[:], ALU.add).then_inc(s_x2h, 1)

            def router(g):
                pool.wait_ge(s_top, GB * (g + 1))
                nc.gpsimd.tensor_tensor(nz[:], top[:, :, 0:2], negc[:], ALU.mult).then_inc(s_nz, 1)
                pool.wait_ge(s_nz, g + 1)
                nc.gpsimd.tensor_tensor(ez[:], powc[:], nz[:], ALU.pow).then_inc(s_ez, 1)
                pool.wait_ge(s_ez, g + 1)
                nc.gpsimd.tensor_tensor(ez1[:], ez[:], onec[:], ALU.add).then_inc(s_ez1, 1)

            def weigh(f, c):
                pool.wait_ge(s_wbs, (CH // 2) * f + (c + 1) // 2)
                pool.wait_ge(s_mul, NF * f + c + 1)
                if c > RING:
                    pool.wait_ge(s_d, NF * f + c - RING + 1)
                nc.gpsimd.tensor_tensor(hid[:, c % RING, :], wbs[:, c - 1, :], mul[:, c % RING, :],
                                        ALU.mult).then_inc(s_hid, 1)

            def turn(g, front=True, ffn=True):
                f = g - 1
                if ffn:
                    weigh(f, 1)
                    weigh(f, 2)
                    weigh(f, 3)
                mix(g)
                if ffn:
                    weigh(f, 4)
                ln2(g)
                if ffn:
                    weigh(f, 5)
                    weigh(f, 6)
                    weigh(f, 7)
                router(g)
                residual(g)

            pool.wait_ge(s_small, 1)
            ln1(0, GB, 1)
            ln1(GB, B, 2)
            pool.wait_ge(s_hi, 3)
            nc.gpsimd.tensor_tensor(wu_lo[:], wu[:], wu_hi[:].bitcast(fp32), ALU.subtract).then_inc(s_lo, 1)
            turn(0, ffn=False)
            with pool.Fori(1, NG - 1) as g:
                turn(g)
            turn(NG - 1, front=False)
            for c in range(1, CH):
                weigh(NG - 1, c)

        @block.scalar
        def _(act):
            act.dma_start(cst[:, 0:256], const_in[:, 0:256]).then_inc(s_cst, 16)
            act.dma_start(bcol[:], bias_col).then_inc(s_bias, 16)
            act.dma_start(brow[:], bias_row.partition_broadcast(128)).then_inc(s_bias, 16)
            act.dma_start(wsh[:], wsh_in[:, 0:128]).then_inc(s_ffn[2], 16)
            act.dma_start(gate_w[:], wsh_in[:, 128:128 + E]).then_inc(s_ffn[3], 16)
            act.dma_start(cst[:, 256:], const_in[:, 256:]).then_inc(s_cst2, 16)
            act.dma_start(wd[0:64, 0, :], wd_in[0:64, :]).then_inc(s_ffn[3], 16)
            act.dma_start(wd[:, 1:NF, :], wd_in[64:64 + CH * 128, :].rearrange("(c p) d -> p c d", p=128)).then_inc(s_ffn[3], 16)

            def t_split(g):
                act.wait_ge(s_t, g + 1)
                if not (isinstance(g, int) and g == 0):
                    act.wait_ge(s_v, GB * g)
                nc.scalar.activation(t_hi[:].rearrange("p s n -> p (s n)"), BQ[:], ACT.Copy).then_inc(s_thi, 1)

            def qk_bias(g):
                act.wait_ge(s_qk, 2 * g + 1)
                for n in (QC, KC):
                    nc.scalar.activation(qk[:, n, :], BQ[:, n * N:(n + 1) * N], ACT.Identity,
                                         bias=bcol[:, n:n + 1]).then_inc(s_qka, 1)

            def exps(g):
                act.wait_ge(s_nmx, g + 1)
                for b in range(GB):
                    for side, k in ((0, C), (1, 128)):
                        nc.scalar.activation(prob[:, b, side, 0:k], BQ[:, (2 * b + side) * 128:(2 * b + side) * 128 + k],
                                             ACT.Exp, bias=nmx[:, b, side:side + 1], scale=SCALE,
                                             accum_out=rsum[:, b, side:side + 1]).then_inc(s_e, 1)

            def pt_copy(g):
                act.wait_ge(s_pt, g + 1)
                nc.scalar.activation(pT[:].rearrange("p b s n -> p (b s n)"), BK[:], ACT.Copy).then_inc(s_pte, 1)

            def gate(g, b):
                act.wait_ge(s_av, GB * g + b + 1)
                nc.scalar.activation(gt[:, b, :], MIXB[b][:, 128:256], ACT.Tanh, scale=-0.5).then_inc(s_g, 1)

            def ht_copy(g):
                act.wait_ge(s_ht, g + 1)
                nc.scalar.activation(hT[:], BT[:, 0:N], ACT.Copy).then_inc(s_hT, 1)

            def ht_split(g):
                nc.scalar.activation(hT_hi[:], BT[:, 0:N], ACT.Copy).then_inc(s_hthi, 1)

            def silu(f, c):
                act.wait_ge(s_gu, NF * f + c + 1)
                p = 64 if c == 0 else 128
                nc.scalar.activation(sil[0:p, c % 2, :], GU[c % 2][0:p, 0:N], ACT.Silu).then_inc(s_sil, 1)

            def weights_copy(f):
                act.wait_ge(s_wtt, f + 1)
                nc.scalar.activation(wT[:], BV[:, 0:N], ACT.Copy).then_inc(s_wT, 1)

            def weights_rows(f, j):
                act.wait_ge(s_wb, (CH // 2) * f + j + 1)
                nc.scalar.activation(wbs[:, 2 * j:2 * j + 2, :].rearrange("p c n -> p (c n)"), WB[:],
                                     ACT.Copy).then_inc(s_wbs, 1)

            def turn(g, front=True, ffn=True):
                f = g - 1
                if ffn:
                    silu(f, 0)
                    silu(f, 1)
                    weights_copy(f)
                    weights_rows(f, 0)
                pt_copy(g)
                if ffn:
                    silu(f, 2)
                    weights_rows(f, 1)
                if ffn:
                    silu(f, 3)
                gate(g, 0)
                gate(g, 1)
                if front:
                    t_split(g + 1)
                if ffn:
                    silu(f, 4)
                    weights_rows(f, 2)
                    silu(f, 5)
                if front:
                    qk_bias(g + 1)
                if ffn:
                    silu(f, 6)
                ht_copy(g)
                if ffn:
                    weights_rows(f, 3)
                    silu(f, 7)
                    silu(f, 8)
                ht_split(g)
                if front:
                    exps(g + 1)

            act.wait_ge(s_bias, 32)
            t_split(0)
            qk_bias(0)
            for n, (w, hi) in enumerate(((wsh, wsh_hi), (wg, wg_hi), (wu, wu_hi))):
                act.wait_ge(s_ffn[(2, 0, 1)[n]], 16)
                nc.scalar.activation(hi[:], w[:], ACT.Copy).then_inc(s_hi, 1)
                if n == 0:
                    act.wait_ge(s_zero, 1)
                    exps(0)
            act.wait_ge(s_cst2, 16)
            nc.scalar.activation(sel[:].rearrange("p c m -> p (c m)"), sel_f, ACT.Copy).then_inc(s_sel, 1)
            turn(0, ffn=False)
            with act.Fori(1, NG - 1) as g:
                turn(g)
            turn(NG - 1, front=False)
            f = NG - 1
            for c in range(NF):
                silu(f, c)
                if c == 1:
                    weights_copy(f)
                if c % 2:
                    weights_rows(f, c // 2)

        @block.vector
        def _(dve):
            def alone(s, value):
                dve.wait_ge(s, value)
                dve.sem_inc(s_waited, 1)

            def ln1_stats(b0, b1):
                for b in range(b0, b1):
                    nc.vector.bn_stats(st1[:, b, :], x_all[:, b, :]).then_inc(s_st1, 1)
                for b in range(b0, b1):
                    dve.wait_ge(s_st1, b + 1)
                    nc.vector.bn_aggr(mv1[:, b, :], st1[:, b, :]).then_inc(s_mv1, 1)

            def ln1_apply(g):
                for b in range(GB):
                    at = g * GB + b
                    nc.vector.tensor_scalar(xn[:, b, :], x_all[:, at, :], mv1[:, at, 0:1], rs1[:, bass.ds(at, 1)],
                                            ALU.subtract, ALU.mult).then_inc(s_xn, 1)

            def t_rest(g):
                dve.wait_ge(s_thi, g + 1)
                nc.vector.tensor_tensor(t_lo[:].rearrange("p s n -> p (s n)"), BQ[:],
                                        t_hi[:].rearrange("p s n -> p (s n)").bitcast(fp32),
                                        ALU.subtract).then_inc(s_tlo, 1)

            def qk_bias(g):
                dve.wait_ge(s_qk, 2 * g + 2)
                for n in (KS, QS):
                    nc.vector.tensor_scalar(qk[:, n, :], BK[:, (n - 2) * N:(n - 1) * N], bcol[:, n:n + 1], None,
                                            ALU.add).then_inc(s_qkd, 1)

            def row_max(g):
                dve.wait_ge(s_s, g + 1)
                sc = BQ[:].rearrange("p (b s k) -> p b s k", b=GB, s=2)
                for side, k in ((0, C), (1, 128)):
                    nc.vector.tensor_reduce(mx[:, :, side], sc[:, :, side, 0:k], AX, ALU.max).then_inc(s_mx, 1)
                dve.wait_ge(s_mx, 2 * (g + 1))
                nc.vector.tensor_scalar(nmx[:], mx[:], -SCALE, None, ALU.mult).then_inc(s_nmx, 1)

            def values(g, b):
                dve.wait_ge(s_v, GB * g + b + 1)
                nc.vector.tensor_tensor(val[:, b, :, :].rearrange("p s n -> p (s n)"), VALB[b][:],
                                        vbias[:].rearrange("p s n -> p (s n)"), ALU.add).then_inc(s_ve, 1)

            def normalise(g):
                dve.wait_ge(s_e, 4 * (g + 1))
                nc.vector.reciprocal(rinv[:], rsum[:]).then_inc(s_ri, 1)
                dve.wait_ge(s_ri, g + 1)
                nc.vector.tensor_tensor(probn[:].rearrange("p b s k -> p (b s) k"),
                                        prob[:].rearrange("p b s k -> p (b s) k"),
                                        rinv[:].rearrange("p b s -> p (b s)").unsqueeze(2).broadcast_to([128, 2 * GB, 128]),
                                        ALU.mult).then_inc(s_pn, 1)

            def mix(g, b):
                dve.wait_ge(s_g, GB * g + b + 1)
                nc.vector.scalar_tensor_tensor(mixd[:, b, :], gt[:, b, :], 1.0, MIXB[b][:, 0:128],
                                               ALU.add, ALU.mult).then_inc(s_md, 1)
                nc.vector.scalar_tensor_tensor(xc[:, b, :], MIXB[b][:, 256:384], -2.0, x_all[:, g * GB + b, :],
                                               ALU.mult, ALU.add).then_inc(s_xc, 1)

            def ln2_stats(g):
                dve.wait_ge(s_x2, g + 1)
                for b in range(GB):
                    nc.vector.bn_stats(st2[:, b, :], x2[:, b, :]).then_inc(s_st2, 1)
                alone(s_st2, GB * (g + 1))
                for b in range(GB):
                    nc.vector.bn_aggr(mv2[:, b, :], st2[:, b, :]).then_inc(s_mv2, 1)

            def ln2_apply(g):
                dve.wait_ge(s_rs2, g + 1)
                if not (isinstance(g, int) and g == 0):
                    dve.wait_ge(s_x2h, g)
                for b in range(GB):
                    nc.vector.tensor_scalar(h[:, b, :], x2[:, b, :], mv2[:, b, 0:1], rs2[:, b:b + 1],
                                            ALU.subtract, ALU.mult).then_inc(s_h, 1)

            def ht_rest(g):
                dve.wait_ge(s_hthi, g + 1)
                nc.vector.tensor_tensor(hT_lo[:], BT[:, 0:N], hT_hi[:].bitcast(fp32),
                                        ALU.subtract).then_inc(s_htlo, 1)

            def router_a(g):
                dve.wait_ge(s_rl, g + 1)
                nc.vector.tensor_tensor(lg[:], BV[:, 0:GB * E].rearrange("p (b e) -> p b e", b=GB),
                                        brow[:, 384:384 + E].unsqueeze(1).broadcast_to([128, GB, E]), ALU.add).then_inc(s_lg, 1)
                alone(s_lg, g + 1)
                for b in range(GB):
                    nc.vector.max(top[:, b, :], lg[:, b, :]).then_inc(s_top, 1)
                alone(s_top, GB * (g + 1))
                for b in range(GB):
                    nc.vector.max_index(topi[:, b, :], top[:, b, :], lg[:, b, :]).then_inc(s_topi, 1)

            def router_b(g):
                dve.wait_ge(s_topi, GB * (g + 1))
                nc.vector.tensor_tensor(oh[:],
                                        iota.unsqueeze(1).unsqueeze(1).broadcast_to([128, GB, 2, E]),
                                        topi[:, :, 0:2].unsqueeze(3).broadcast_to([128, GB, 2, E]),
                                        ALU.is_equal).then_inc(s_oh, 1)
                dve.wait_ge(s_ez1, g + 1)
                nc.vector.reciprocal(sg[:], ez1[:]).then_inc(s_sg, 1)
                dve.wait_ge(s_sg, g + 1)
                nc.vector.tensor_tensor(sgs[:], sg[:, :, 0], sg[:, :, 1], ALU.add).then_inc(s_sgs, 1)
                dve.wait_ge(s_sgs, g + 1)
                nc.vector.reciprocal(sgr[:], sgs[:]).then_inc(s_sgr, 1)
                dve.wait_ge(s_sgr, g + 1)
                nc.vector.tensor_tensor(wt[:], sg[:], sgr[:].unsqueeze(2).broadcast_to([128, GB, 2]), ALU.mult).then_inc(s_wt, 1)
                dve.wait_ge(s_oh, g + 1)
                dve.wait_ge(s_wt, g + 1)
                nc.vector.tensor_tensor(ohw[:], oh[:], wt[:].unsqueeze(3).broadcast_to([128, GB, 2, E]), ALU.mult).then_inc(s_ohw, 1)
                dve.wait_ge(s_ohw, g + 1)
                nc.vector.tensor_tensor(wsum[:], ohw[:, :, 0, :], ohw[:, :, 1, :], ALU.add).then_inc(s_ws, 1)
                nc.vector.tensor_tensor(wst_r[:, :, 0:E], ohw[:, :, 0, :], ohw[:, :, 1, :], ALU.add).then_inc(s_whi, 1)
                dve.wait_ge(s_ws, g + 1)
                dve.wait_ge(s_whi, g + 1)
                nc.vector.tensor_tensor(wst_r[:, :, E:2 * E], wsum[:], wst[:, :, 0:E], ALU.subtract).then_inc(s_wlo, 1)

            def up_mul(f, c):
                dve.wait_ge(s_sil, NF * f + c + 1)
                if c == 0:
                    nc.vector.tensor_tensor(hid0[0:64, :], GU[0][64:128, 0:N], sil[0:64, 0, :], ALU.mult)\
                      .then_inc(s_mul, 1)
                    return
                if c > RING:
                    dve.wait_ge(s_hid, (CH - 1) * f + c - RING)
                nc.vector.tensor_tensor(mul[:, c % RING, :], GU[c % 2][:, N:2 * N], sil[:, c % 2, :], ALU.mult)\
                  .then_inc(s_mul, 1)

            def weigh_last(f):
                dve.wait_ge(s_wbs, (CH // 2) * (f + 1))
                dve.wait_ge(s_mul, NF * (f + 1))
                dve.wait_ge(s_d, NF * f + NF - RING)
                nc.vector.tensor_tensor(hid[:, CH % RING, :], wbs[:, CH - 1, :], mul[:, CH % RING, :],
                                        ALU.mult).then_inc(s_hidl, 1)

            def finish(f):
                dve.wait_ge(s_d, NF * (f + 1))
                dve.wait_ge(s_x2h, f + 1)
                dve.wait_ge(s_out, 16 * (f + 1))
                nc.vector.tensor_tensor(yout[:].rearrange("p b d -> p (b d)"), Y[:, 0:N],
                                        x2h[:].rearrange("p b d -> p (b d)"), ALU.add).then_inc(s_y, 1)

            def turn(g, front=True, ffn=True):
                f = g - 1
                if ffn:
                    up_mul(f, 0)
                normalise(g)
                values(g, 0)
                if ffn:
                    up_mul(f, 1)
                values(g, 1)
                if front:
                    ln1_apply(g + 1)
                if ffn:
                    up_mul(f, 2)
                    up_mul(f, 3)
                mix(g, 0)
                mix(g, 1)
                if front:
                    t_rest(g + 1)
                ln2_stats(g)
                if ffn:
                    up_mul(f, 4)
                    up_mul(f, 5)
                if front:
                    qk_bias(g + 1)
                ln2_apply(g)
                if ffn:
                    up_mul(f, 6)
                if front:
                    row_max(g + 1)
                if ffn:
                    up_mul(f, 7)
                router_a(g)
                if ffn:
                    up_mul(f, 8)
                    weigh_last(f)
                ht_rest(g)
                router_b(g)
                if ffn:
                    finish(f)

            dve.sem_inc(s_y, 1)
            nc.vector.memset(ctx_t[96:128, :, :], 0.0).then_inc(s_pad, 1)
            nc.vector.memset(wd[64:128, 0, :], 0.0).then_inc(s_pad, 1)
            dve.wait_ge(s_xin[0], 16)
            ln1_stats(0, GB)
            dve.wait_ge(s_rs1, 1)
            ln1_apply(0)
            dve.wait_ge(s_aw[0], 16)
            nc.vector.tensor_copy(wqk_hi[:], aw[:, 0:4, :]).then_inc(s_qkw, 1)
            dve.wait_ge(s_qkw, 1)
            nc.vector.tensor_tensor(wqk_lo[:], aw[:, 0:4, :], wqk_hi[:].bitcast(fp32), ALU.subtract).then_inc(s_qkw, 1)
            t_rest(0)
            dve.wait_ge(s_xin[1], 16)
            ln1_stats(GB, B)
            dve.wait_ge(s_aw[1], 16)
            nc.vector.tensor_scalar(wv[:, 0, 0:128], aw[:, 4, :], -0.5, None, ALU.mult).then_inc(s_wv, 1)
            nc.vector.tensor_scalar(wv[:, 1, 0:128], aw[:, 5, :], 0.5, None, ALU.mult).then_inc(s_wv, 1)
            dve.wait_ge(s_bias, 32)
            qk_bias(0)
            row_max(0)
            dve.wait_ge(s_prod, 1)
            nc.vector.tensor_copy(wv[:, :, 128:256], GU[0][:, 0:256].rearrange("p (s n) -> p s n", s=2)).then_inc(s_wv, 1)
            dve.wait_ge(s_wv, 3)
            nc.vector.tensor_copy(wv_hi[:], wv[:]).then_inc(s_wvs, 1)
            dve.wait_ge(s_wvs, 1)
            nc.vector.tensor_tensor(wv_lo[:], wv[:], wv_hi[:].bitcast(fp32), ALU.subtract).then_inc(s_wvs, 1)
            nc.vector.tensor_scalar(vbias[:, 0, 0:128], brow[:, 0:128], -0.5, None, ALU.mult).then_inc(s_vb, 1)
            nc.vector.tensor_scalar(vbias[:, 1, 0:128], brow[:, 128:256], 0.5, None, ALU.mult).then_inc(s_vb, 1)
            nc.vector.tensor_tensor(vbias[:, 0, 128:256], GU[0][:, 256:384], brow[:, 256:384], ALU.add).then_inc(s_vb, 1)
            nc.vector.tensor_copy(vbias[:, 1, 128:256], GU[0][:, 384:512]).then_inc(s_vb, 1)
            for n, (w, hi, lo) in enumerate(((wsh, wsh_hi, wsh_lo), (wg, wg_hi, wg_lo))):
                dve.wait_ge(s_hi, n + 1)
                nc.vector.tensor_tensor(lo[:], w[:], hi[:].bitcast(fp32), ALU.subtract).then_inc(s_lo, 1)
            dve.wait_ge(s_vb, 4)
            dve.wait_ge(s_rs1, 2)
            turn(0, ffn=False)
            dve.wait_ge(s_cst2, 16)
            with dve.Fori(1, NG - 1) as g:
                turn(g)
            turn(NG - 1, front=False)
            f = NG - 1
            up_mul(f, 0)
            up_mul(f, 1)
            for c in range(2, NF):
                up_mul(f, c)
            weigh_last(f)
            finish(f)

        @block.tensor
        def _(pe):
            mm = nc.tensor.matmul

            def split3(dst, w_hi, w_lo, r_hi, r_lo):
                mm(dst, w_hi, r_hi, start=True, stop=False)
                mm(dst, w_hi, r_lo, start=False, stop=False)
                return mm(dst, w_lo, r_hi, start=False, stop=True)

            def transpose_in(g):
                pe.wait_ge(s_xn, GB * (g + 1))
                pe.wait_ge(s_ctx, 16 * (g + 1))
                for b in range(GB):
                    nc.tensor.transpose(BQ[:, b * 128:(b + 1) * 128], xn[:, b, :], ident)
                for b in range(GB):
                    last = nc.tensor.transpose(BQ[:, N + b * 128:N + (b + 1) * 128], ctx_t[:, b, :], ident)
                last.then_inc(s_t, 1)

            def project(g):
                pe.wait_ge(s_thi, g + 1)
                pe.wait_ge(s_tlo, g + 1)
                for n in range(4):
                    side, dst = n // 2, (BQ, BK)[n // 2][:, (n % 2) * N:(n % 2 + 1) * N]
                    last = split3(dst, wqk_hi[:, n, :], wqk_lo[:, n, :], t_hi[:, side, :], t_lo[:, side, :])
                    if n % 2:
                        last.then_inc(s_qk, 1)

            def scores(g):
                pe.wait_ge(s_qka, 2 * (g + 1))
                pe.wait_ge(s_qkd, 2 * (g + 1))
                for b in range(GB):
                    at = slice(b * 128, (b + 1) * 128)
                    mm(BQ[:, b * 256:b * 256 + C], qk[:, QC, at], qk[:, KS, b * 128:b * 128 + C], start=True, stop=True)
                    last = mm(BQ[:, b * 256 + 128:b * 256 + 256], qk[:, QS, at], qk[:, KC, at], start=True, stop=True)
                last.then_inc(s_s, 1)

            def values(g, b):
                for side in range(2):
                    at = slice(b * 128, (b + 1) * 128)
                    last = split3(VALB[b][:, side * 256:(side + 1) * 256], t_hi[:, 1 - side, at], t_lo[:, 1 - side, at],
                                  wv_hi[:, side, :], wv_lo[:, side, :])
                last.then_inc(s_v, 1)

            def probs_t(g):
                pe.wait_ge(s_pn, g + 1)
                pe.wait_ge(s_ve, GB * g + 1)
                for b in range(GB):
                    nc.tensor.transpose(BK[:, b * 256:b * 256 + 128], probn[:, b, 0, :], ident)
                    last = mm(BK[:, b * 256 + 128:b * 256 + 256], probn[0:C, b, 1, :], interpT[0:C, :],
                              start=True, stop=True)
                last.then_inc(s_pt, 1)

            def mix(g, b):
                if b == 0:
                    pe.wait_ge(s_pte, g + 1)
                    pe.wait_ge(s_ve, GB * (g + 1))
                mm(MIXB[b][:, 0:256], pT[0:C, b, 0, :], val[0:C, b, 0, :], start=True, stop=False)
                mm(MIXB[b][:, 0:256], pT[:, b, 1, :], val[:, b, 1, :], start=False, stop=True)
                mm(MIXB[b][:, 256:384], pT[0:C, b, 0, :], val[0:C, b, 0, 0:128], start=True, stop=True)\
                  .then_inc(s_av, 1)

            def transpose_h(g):
                pe.wait_ge(s_h, GB * (g + 1))
                for b in range(GB):
                    last = nc.tensor.transpose(BT[:, b * 128:(b + 1) * 128], h[:, b, :], ident)
                last.then_inc(s_ht, 1)

            def logits(g):
                pe.wait_ge(s_hT, g + 1)
                for b in range(GB):
                    last = mm(BV[:, b * E:(b + 1) * E], hT[:, b * 128:(b + 1) * 128], gate_w[:], start=True, stop=True)
                last.then_inc(s_rl, 1)

            def weights_t(f):
                pe.wait_ge(s_wlo, f + 1)
                for b in range(GB):
                    last = nc.tensor.transpose(BV[:, b * 128:(b + 1) * 128], wst[:, b, :], ident)
                last.then_inc(s_wtt, 1)

            def gate_up(f, c):
                if c == 0:
                    pe.wait_ge(s_hthi, f + 1)
                    pe.wait_ge(s_htlo, f + 1)
                if c >= 2:
                    pe.wait_ge(s_mul, NF * f + c - 1)
                if c == 0:
                    split3(GU[0][:, 0:N], wsh_hi[:], wsh_lo[:], hT_hi[:], hT_lo[:]).then_inc(s_gu, 1)
                    return
                at = slice((c - 1) * 128, c * 128)
                split3(GU[c % 2][:, 0:N], wg_hi[:, at], wg_lo[:, at], hT_hi[:], hT_lo[:])
                split3(GU[c % 2][:, N:2 * N], wu_hi[:, at], wu_lo[:, at], hT_hi[:], hT_lo[:]).then_inc(s_gu, 1)

            def spread(f, j):
                if j == 0:
                    pe.wait_ge(s_wT, f + 1)
                else:
                    pe.wait_ge(s_wbs, (CH // 2) * f + j)
                for i in range(2):
                    last = mm(WB[:, i * N:(i + 1) * N], sel[:, 2 * j + i, :], wT[:], start=True, stop=True)
                last.then_inc(s_wb, 1)

            def down(f, c):
                if c == 0:
                    pe.wait_ge(s_mul, NF * f + 1)
                    pe.wait_ge(s_y, f + 1)
                elif c == CH:
                    pe.wait_ge(s_hidl, f + 1)
                else:
                    pe.wait_ge(s_hid, (CH - 1) * f + c)
                src = hid0[:] if c == 0 else hid[:, c % RING, :]
                for b in range(GB):
                    last = mm(Y[:, b * 128:(b + 1) * 128], src[:, b * 128:(b + 1) * 128], wd[:, c, :],
                              start=(c == 0 and b == 0), stop=(c == NF - 1), skip_group_check=True)
                last.then_inc(s_d, 1)

            def turn(g, front=True):
                f = g - 1
                gate_up(f, 0)
                gate_up(f, 1)
                values(g, 0)
                values(g, 1)
                weights_t(f)
                gate_up(f, 2)
                down(f, 0)
                spread(f, 0)
                probs_t(g)
                gate_up(f, 3)
                spread(f, 1)
                down(f, 1)
                mix(g, 0)
                mix(g, 1)
                if front:
                    transpose_in(g + 1)
                gate_up(f, 4)
                down(f, 2)
                spread(f, 2)
                gate_up(f, 5)
                down(f, 3)
                if front:
                    project(g + 1)
                gate_up(f, 6)
                down(f, 4)
                spread(f, 3)
                transpose_h(g)
                if front:
                    scores(g + 1)
                gate_up(f, 7)
                logits(g)
                gate_up(f, 8)
                for c in range(5, NF):
                    down(f, c)

            pe.wait_ge(s_cst, 16)
            pe.wait_ge(s_pad, 2)
            transpose_in(0)
            pe.wait_ge(s_qkw, 2)
            project(0)
            pe.wait_ge(s_aw[1], 16)
            pe.wait_ge(s_bias, 32)
            for side in range(2):
                mm(GU[0][:, side * 128:(side + 1) * 128], aw[:, 6 + side, :], aw[:, 8 + side, :], start=True, stop=True)
            for side in range(2):
                last = mm(GU[0][:, 256 + side * 128:384 + side * 128], bcol[:, 4 + side:5 + side].broadcast_to([128, 128]),
                          aw[:, 8 + side, :], start=True, stop=True)
            last.then_inc(s_prod, 1)
            scores(0)
            pe.wait_ge(s_wvs, 2)
            values(0, 0)
            values(0, 1)
            probs_t(0)
            transpose_in(1)
            mix(0, 0)
            mix(0, 1)
            project(1)
            scores(1)
            transpose_h(0)
            pe.wait_ge(s_ffn[3], 48)
            logits(0)
            pe.wait_ge(s_lo, 3)
            pe.wait_ge(s_sel, 1)
            pe.wait_ge(s_vb, 4)
            with pe.Fori(1, NG - 1) as g:
                turn(g)
            turn(NG - 1, front=False)
            f = NG - 1
            gate_up(f, 0)
            gate_up(f, 1)
            weights_t(f)
            down(f, 0)
            gate_up(f, 2)
            spread(f, 0)
            gate_up(f, 3)
            for c in range(4, NF):
                down(f, c - 3)
                gate_up(f, c)
                if c % 2:
                    spread(f, (c - 3) // 2)
            spread(f, 3)
            for c in range(NF - 3, NF):
                down(f, c)


def kernel(x, ctx_1024, L0_xattn_Wq_c, L0_xattn_bq_c, L0_xattn_Wk_s, L0_xattn_bk_s, L0_xattn_Wv_s, L0_xattn_bv_s,
           L0_xattn_Wq_s, L0_xattn_bq_s, L0_xattn_Wk_c, L0_xattn_bk_c, L0_xattn_Wv_c, L0_xattn_bv_c, L0_xattn_Wg,
           L0_xattn_bg, L0_ffn_gate_w, L0_ffn_gate_b, L0_ffn_shared_wg, L0_ffn_shared_wu, L0_ffn_shared_wd,
           L0_ffn_experts_wg, L0_ffn_experts_wu, L0_ffn_experts_wd):
    import numpy as np
    import concourse.bacc as bacc
    from concourse.bass_utils import run_bass_kernel_spmd

    def arr(a):
        return np.ascontiguousarray(a)

    x, ctx_1024 = arr(x), arr(ctx_1024)
    D, C = x.shape[2], ctx_1024.shape[1]
    T = x.shape[1]
    E = L0_ffn_gate_w.shape[1]
    H = L0_ffn_shared_wg.shape[1]
    wg_gate = arr(L0_xattn_Wg)
    attn_w = arr(np.concatenate([arr(L0_xattn_Wq_c).T, arr(L0_xattn_Wk_c).T, arr(L0_xattn_Wk_s).T, arr(L0_xattn_Wq_s).T,
                                 arr(L0_xattn_Wv_s).T, arr(L0_xattn_Wv_c).T, arr(L0_xattn_Wv_s), arr(L0_xattn_Wv_c),
                                 wg_gate[:, :D].T, wg_gate[:, D:].T], axis=1))
    bias_col = arr(np.stack([arr(b) for b in (L0_xattn_bq_c, L0_xattn_bk_c, L0_xattn_bk_s, L0_xattn_bq_s,
                                              L0_xattn_bv_s, L0_xattn_bv_c)], axis=1))
    bias_row = arr(np.concatenate([arr(L0_xattn_bv_s), arr(L0_xattn_bv_c), arr(L0_xattn_bg), arr(L0_ffn_gate_b)]))
    wg = arr(np.transpose(arr(L0_ffn_experts_wg), (1, 0, 2)).reshape(D, E * H))
    wu = arr(np.transpose(arr(L0_ffn_experts_wu), (1, 0, 2)).reshape(D, E * H))
    wsh = arr(np.concatenate([arr(L0_ffn_shared_wg), arr(L0_ffn_shared_wu), arr(L0_ffn_gate_w)], axis=1))
    wd = arr(np.concatenate([arr(L0_ffn_shared_wd), arr(L0_ffn_experts_wd).reshape(E * H, D)], axis=0))

    consts = np.zeros((128, 256 + (E * H // 128) * 128 + E), np.float32)
    consts[:, 0:128] = np.eye(128, dtype=np.float32)
    pos = np.clip((np.arange(T, dtype=np.float32) + np.float32(0.5)) * np.float32(C / T) - np.float32(0.5), 0, C - 1)
    lo = np.floor(pos).astype(np.int32)
    for t in range(T):
        w = pos[t] - np.float32(lo[t])
        consts[lo[t], 128 + t] += 1 - w
        consts[min(lo[t] + 1, C - 1), 128 + t] += w
    for c in range(E * H // 128):
        for m in range(128):
            e = (128 * c + m) // H
            consts[e, 256 + 128 * c + m] = 1
            consts[E + e, 256 + 128 * c + m] = 1
    consts[:, -E:] = np.arange(E, dtype=np.float32)

    arrays = dict(x=x, ctx_in=ctx_1024, attn_w=attn_w, bias_col=bias_col, bias_row=bias_row, const_in=consts,
                  wg_in=wg, wu_in=wu, wsh_in=wsh, wd_in=wd)
    nc = bacc.Bacc("TRN2", target_bir_lowering=False, num_devices=1)
    args = [nc.dram_tensor(name, a.shape, mybir.dt.from_np(a.dtype), kind="ExternalInput").ap()
            for name, a in arrays.items()]
    out = nc.dram_tensor("out", x.shape, mybir.dt.float32, kind="ExternalOutput").ap()
    xattn_ffn_kernel(nc, *args, out)
    return run_bass_kernel_spmd(nc, [arrays], core_ids=[0]).results[0]["out"]
```

```python
import concourse.bass as bass
import numpy as np
from concourse import mybir
from contextlib import ExitStack




def xattn_ffn_kernel(nc, x, ctx_in, attn_w, bias_col, bias_row, const_in, wg_in, wu_in, wsh_in, wd_in, out):
    fp32, f32r, u32 = mybir.dt.float32, mybir.dt.float32r, mybir.dt.uint32
    ALU = mybir.AluOpType
    ACT = mybir.ActivationFunctionType
    AX = mybir.AxisListType.X

    B, T, D = x.shape
    C = ctx_in.shape[1]
    GB = 2
    NG = B // GB
    N = GB * T
    E = 16
    H = 64
    CH = E * H // 128
    NF = CH + 1
    GR = 3
    RING = 4
    SCALE = float(D) ** -0.5
    EPS = 1e-5
    WARM_UP = 11
    BRIDGES = 8, 1, 9
    QC, KC, KS, QS = range(4)

    ctx = ExitStack()
    with ctx:
        def sb(name, shape, dt=fp32):
            return ctx.enter_context(nc.sbuf_tensor(name, shape, dt))

        def pb(name):
            return ctx.enter_context(nc.psum_tensor(name, [128, 512], fp32))

        def sem(name):
            return ctx.enter_context(nc.semaphore(name))

        aw = sb("aw", [128, 10, 128])
        bcol = sb("bcol", [128, 6])
        brow = sb("brow", [128, 3 * 128 + E])
        cst = sb("cst", [128, 2 * 128 + CH * 128 + E])
        ident = cst[:, 0:128]
        interpT = cst[:, 128:256]
        sel_f = cst[:, 256:256 + CH * 128]
        iota = cst[:, 256 + CH * 128:]
        wqk_hi = sb("wqk_hi", [128, 4, 128], f32r)
        wqk_lo = sb("wqk_lo", [128, 4, 128], f32r)
        wv = sb("wv", [128, 2, 256])
        wv_hi = sb("wv_hi", [128, 2, 256], f32r)
        wv_lo = sb("wv_lo", [128, 2, 256], f32r)
        vbias = sb("vbias", [128, 2, 256])
        wg = sb("wg", [128, E * H])
        wu = sb("wu", [128, E * H])
        wsh = sb("wsh", [128, 128])
        wg_hi = sb("wg_hi", [128, E * H], f32r)
        wg_lo = sb("wg_lo", [128, E * H], f32r)
        wu_hi = sb("wu_hi", [128, E * H], f32r)
        wu_lo = sb("wu_lo", [128, E * H], f32r)
        wsh_hi = sb("wsh_hi", [128, 128], f32r)
        wsh_lo = sb("wsh_lo", [128, 128], f32r)
        wd = sb("wd", [128, NF, 128])
        gate_w = sb("gate_w", [128, E])
        sel = sb("sel", [128, CH, 128], f32r)
        inv_e = sb("inv_e", [128, GB, 2])
        onec = sb("onec", [128, GB, 2])
        epsc = sb("epsc", [128, B])
        halfc = sb("halfc", [128, B])

        x_all = sb("x_all", [128, B, 128])
        ctx_t = sb("ctx_t", [128, GB, 128])
        st1 = sb("st1", [128, B, 6])
        mv1 = sb("mv1", [128, B, 2])
        ve1 = sb("ve1", [128, B])
        rs1 = sb("rs1", [128, B])
        xn = sb("xn", [128, GB, 128])
        t_hi = sb("t_hi", [128, 2, N], f32r)
        t_lo = sb("t_lo", [128, 2, N], f32r)
        t_first = sb("t_first", [128, 2, N])
        qk = sb("qk", [128, 4, N])
        val = sb("val", [128, GB, 2, 256])
        mx = sb("mx", [128, GB, 2])
        nmx = sb("nmx", [128, GB, 2])
        prob = sb("prob", [128, GB, 2, 128])
        rsum = sb("rsum", [128, GB, 2])
        rinv = sb("rinv", [128, GB, 2])
        probn = sb("probn", [128, GB, 2, 128])
        pT = sb("pT", [128, GB, 2, 128])
        gt = sb("gt", [128, GB, 128])
        c2s = sb("c2s", [128, GB, 128])
        s2c = sb("s2c", [128, GB, 128])
        xc = sb("xc", [128, GB, 128])
        x2 = sb("x2", [128, GB, 128])
        st2 = sb("st2", [128, GB, 6])
        mv2 = sb("mv2", [128, GB, 2])
        ve2 = sb("ve2", [128, GB])
        rs2 = sb("rs2", [128, GB])
        h = sb("h", [128, GB, 128])
        x2h = sb("x2h", [128, GB, 128])
        hT = sb("hT", [128, N])
        hT_hi = sb("hT_hi", [128, N], f32r)
        hT_lo = sb("hT_lo", [128, N], f32r)
        lg = sb("lg", [128, GB, E])
        top = sb("top", [128, GB, 8])
        topi = sb("topi", [128, GB, 8], u32)
        ez = sb("ez", [128, GB, 2])
        ez1 = sb("ez1", [128, GB, 2])
        sg = sb("sg", [128, GB, 2])
        sgs = sb("sgs", [128, GB])
        sgr = sb("sgr", [128, GB])
        wt = sb("wt", [128, GB, 2])
        oh = sb("oh", [128, GB, 2, E])
        ohw = sb("ohw", [128, GB, 2, E])
        wsum = sb("wsum", [128, GB, E])
        wst = sb("wst", [128, GB, 128])
        wst_r = wst[:].bitcast(f32r)
        wT = sb("wT", [128, N], f32r)
        sil = sb("sil", [128, GR, N])
        mul = sb("mul", [128, RING, N])
        wbs = sb("wbs", [128, CH, N])
        hid = sb("hid", [128, RING, N])
        hid0 = sb("hid0", [128, N])
        yout = sb("yout", [128, GB, 128])
        table_in = sb("table_in", [128, 2])
        warm_up = sb("warm_up", [128, 128])

        GU = [pb(f"GU{i}") for i in range(GR)]
        Y = pb("Y")
        BQ = pb("BQ")
        BK = pb("BK")
        BT = pb("BT")
        BV = pb("BV")
        VALB = [BK, BT]
        MIXB = [BT, BV]

        def mix_bank(g, b):
            return BQ if b == 1 and isinstance(g, int) and g == NG - 1 else MIXB[b]

        FIRSTB = [BQ, GU[0], BK, GU[1]]
        SPREADB = [BV, BK, BT, BQ]

        s_cst, s_cst2, s_bias, s_ctx, s_out = (sem(n) for n in
            ("identity_in", "selection_in", "bias_in", "ctx_in_sem", "out_stored"))
        s_aw = [sem("qk_w_in"), sem("value_w_in")]
        s_ffn = [sem(n) for n in ("gate_w_in", "up_w_in", "shared_w_in", "router_down_w_in")]
        s_small = sem("small_consts_set")
        s_hi, s_lo, s_sel = sem("ffn_hi_parts"), sem("ffn_lo_parts"), sem("selection_ready")
        s_xin = [sem(f"x_in_{i}") for i in range(3)]
        s_zero = sem("zeros_set")
        s_warm = sem("warm_up_set")
        s_pad = sem("row_padding_set")
        s_qkw = sem("qk_weights_split")
        s_prod = sem("value_gate_products")
        s_wv = sem("value_weights_built")
        s_wvs = sem("value_weights_split")
        s_vb = sem("value_bias_built")
        s_st1, s_mv1, s_ve1, s_rs1, s_xn = (sem(n) for n in ("stats1", "meanvar1", "vareps1", "rstd1", "xn_ready"))
        s_t, s_thi, s_tlo = sem("transposed"), sem("t_hi_ready"), sem("t_lo_ready")
        s_tf = sem("t_first_ready")
        s_qkf = sem("first_qk_projected")
        s_qk, s_qka, s_qkd = sem("qk_projected"), sem("qk_x_ready"), sem("qk_ctx_ready")
        s_s, s_mx, s_nmx, s_e, s_ri, s_pn = (sem(n) for n in
            ("scores_done", "row_max", "neg_max", "exp_done", "inv_sum", "probs_normed"))
        s_v, s_ve = sem("values_projected"), sem("values_ready")
        s_pt, s_pte = sem("probs_transposed"), sem("pT_ready")
        s_av, s_g, s_c2s, s_s2c, s_xc, s_x2 = (sem(n) for n in
            ("mix_products", "gate_tanh", "c2s_gated", "s2c_gated", "mix_base", "x2_ready"))
        s_st2, s_mv2, s_ve2, s_rs2, s_h, s_x2h = (sem(n) for n in
            ("stats2", "meanvar2", "vareps2", "rstd2", "h_ready", "x2h_ready"))
        s_hT = sem("hT_ready")
        s_ht, s_hthi, s_htlo = sem("h_transposed"), sem("hT_hi_ready"), sem("hT_lo_ready")
        s_rl, s_lg, s_top, s_topi, s_ez, s_ez1 = (sem(n) for n in
            ("router_logits", "logits_biased", "top8", "top8_index", "exp_neg_logit", "one_plus_exp"))
        s_sg, s_sgs, s_sgr, s_wt, s_oh, s_ohw, s_ws, s_whi, s_wlo = (sem(n) for n in
            ("sigmoid", "sigmoid_sum", "sigmoid_inv", "top2_weights", "one_hot", "one_hot_weighted",
             "weights_row", "weights_hi", "weights_lo"))
        s_wtt, s_wT = sem("weights_transposed"), sem("wT_ready")
        s_gu, s_sil, s_mul, s_wb, s_wbs, s_hid, s_hidl, s_d = (sem(n) for n in
            ("gate_up_done", "silu_done", "mul_done", "weights_spread", "weights_on_rows", "hidden_ready",
             "last_hidden_ready", "down_done"))
        s_y = sem("y_ready")
        s_waited = sem("waits_alone")

        block = ctx.enter_context(nc.Block())


        @block.sync
        def _(sp):
            sp.sem_inc(s_out, 16)

            def load_ctx(g):
                sp.wait_ge(s_t, g)
                sp.dma_start(ctx_t[0:C, :, :],
                             ctx_in[bass.ds(g * GB, GB)].rearrange("b p d -> p b d")).then_inc(s_ctx, 16)

            sp.dma_start(x_all[:, 0:GB, :], x[0:GB].rearrange("b p d -> p b d")).then_inc(s_xin[0], 16)
            sp.wait_ge(s_pad, 1)
            sp.dma_start(ctx_t[0:C, :, :], ctx_in[0:GB].rearrange("b p d -> p b d")).then_inc(s_ctx, 16)
            sp.dma_start(aw[:, 4:10, :], attn_w[:, 512:1280].rearrange("p (n d) -> p n d", n=6)).then_inc(s_aw[1], 16)
            sp.dma_start(bcol[:], bias_col).then_inc(s_bias, 16)
            sp.dma_start(brow[:], bias_row.partition_broadcast(128)).then_inc(s_bias, 16)
            sp.dma_start(x_all[:, GB:2 * GB, :], x[GB:2 * GB].rearrange("b p d -> p b d")).then_inc(s_xin[1], 16)
            sp.dma_start(wsh[:], wsh_in[:, 0:128]).then_inc(s_ffn[2], 16)
            sp.dma_start(x_all[:, 2 * GB:B, :], x[2 * GB:B].rearrange("b p d -> p b d")).then_inc(s_xin[2], 16)
            load_ctx(1)
            sp.dma_start(wg[:], wg_in).then_inc(s_ffn[0], 16)
            sp.dma_start(wu[:], wu_in).then_inc(s_ffn[1], 16)
            sp.dma_start(gate_w[:], wsh_in[:, 128:128 + E]).then_inc(s_ffn[3], 16)
            sp.dma_start(cst[:, 256:], const_in[:, 256:]).then_inc(s_cst2, 16)
            sp.dma_start(wd[0:64, 0, :], wd_in[0:64, :]).then_inc(s_ffn[3], 16)
            sp.dma_start(wd[:, 1:NF, :], wd_in[64:64 + CH * 128, :].rearrange("(c p) d -> p c d", p=128)).then_inc(s_ffn[3], 16)

            def store(g):
                sp.wait_ge(s_y, g + 2)
                sp.dma_start(out[bass.ds(g * GB, GB)].rearrange("b p d -> p b d"), yout[:]).then_inc(s_out, 16)

            load_ctx(2)
            with sp.Fori(1, NG - 2) as g:
                load_ctx(g + 2)
                store(g - 1)
            for g in range(NG - 3, NG):
                store(g)
            sp.wait_ge(s_out, 16 * (NG + 1))

        @block.gpsimd
        def _(pool):
            nc.gpsimd.memset(halfc[:], -0.5)
            nc.gpsimd.memset(inv_e[:], float(np.exp(-1.0)))
            nc.gpsimd.memset(onec[:], 1.0)
            nc.gpsimd.memset(epsc[:], EPS).then_inc(s_small, 1)
            nc.gpsimd.memset(prob[:], 0.0)
            nc.gpsimd.memset(wst[:], 0.0)
            nc.gpsimd.memset(hid0[:], 0.0).then_inc(s_zero, 1)

            def ln1(g0, g1):
                at = slice(g0 * GB, g1 * GB)
                pool.wait_ge(s_mv1, g1 * GB)
                nc.gpsimd.tensor_tensor(ve1[:, at], mv1[:, at, 1], epsc[:, at], ALU.add).then_inc(s_ve1, g1 - g0)
                pool.wait_ge(s_ve1, g1)
                nc.gpsimd.tensor_tensor(rs1[:, at], ve1[:, at], halfc[:, at], ALU.pow).then_inc(s_rs1, g1 - g0)

            def ln2(g):
                pool.wait_ge(s_mv2, GB * (g + 1))
                nc.gpsimd.tensor_tensor(ve2[:], mv2[:, :, 1], epsc[:, 0:GB], ALU.add).then_inc(s_ve2, 1)
                pool.wait_ge(s_ve2, g + 1)
                nc.gpsimd.tensor_tensor(rs2[:], ve2[:], halfc[:, 0:GB], ALU.pow).then_inc(s_rs2, 1)

            def mix(g):
                pool.wait_ge(s_s2c, GB * (g + 1))
                pool.wait_ge(s_xc, GB * (g + 1))
                pool.wait_ge(s_x2h, g)
                nc.gpsimd.tensor_tensor(x2[:], s2c[:], xc[:], ALU.add).then_inc(s_x2, 1)

            def residual(g):
                pool.wait_ge(s_y, g + 1)
                pool.wait_ge(s_h, GB * (g + 1))
                nc.gpsimd.tensor_tensor(x2h[:], x2[:], h[:], ALU.add).then_inc(s_x2h, 1)

            def router(g):
                pool.wait_ge(s_top, GB * (g + 1))
                nc.gpsimd.tensor_tensor(ez[:], inv_e[:], top[:, :, 0:2], ALU.pow).then_inc(s_ez, 1)
                pool.wait_ge(s_ez, g + 1)
                nc.gpsimd.tensor_tensor(ez1[:], ez[:], onec[:], ALU.add).then_inc(s_ez1, 1)

            def weigh(f, c):
                pool.wait_ge(s_wbs, (CH // 2) * f + (c + 1) // 2)
                pool.wait_ge(s_mul, NF * f + c + 1)
                if c > RING:
                    pool.wait_ge(s_d, NF * f + c - RING + 1)
                nc.gpsimd.tensor_tensor(hid[:, c % RING, :], wbs[:, c - 1, :], mul[:, c % RING, :],
                                        ALU.mult).then_inc(s_hid, 1)

            def turn(g, front=True):
                f = g - 1
                weigh(f, 1)
                weigh(f, 2)
                weigh(f, 3)
                weigh(f, 4)
                if front:
                    mix(g)
                ln2(g)
                weigh(f, 5)
                weigh(f, 6)
                weigh(f, 7)
                router(g)
                residual(g)

            pool.wait_ge(s_small, 1)
            ln1(0, 1)
            ln1(1, 2)
            for n, (w, hi, lo) in enumerate(((wg, wg_hi, wg_lo), (wu, wu_hi, wu_lo))):
                pool.wait_ge(s_hi, n + 2)
                nc.gpsimd.tensor_tensor(lo[:], w[:], hi[:].bitcast(fp32), ALU.subtract).then_inc(s_lo, 1)
            ln2(0)
            ln1(2, 6)
            router(0)
            residual(0)
            ln1(6, NG)
            with pool.Fori(1, NG - 1) as g:
                turn(g)
            turn(NG - 1, front=False)
            for c in range(1, CH):
                weigh(NG - 1, c)

        @block.scalar
        def _(act):
            act.dma_start(cst[:, 0:256], const_in[:, 0:256]).then_inc(s_cst, 16)
            act.dma_start(aw[:, 0:4, :], attn_w[:, 0:512].rearrange("p (n d) -> p n d", n=4)).then_inc(s_aw[0], 16)

            def t_split(g):
                act.wait_ge(s_t, g + 1)
                act.wait_ge(s_v, GB * g)
                nc.scalar.activation(t_hi[:].rearrange("p s n -> p (s n)"), BQ[:], ACT.Copy).then_inc(s_thi, 1)

            def qk_bias(g):
                act.wait_ge(s_qk, 2 * g + 1)
                for n in (QC, KC):
                    nc.scalar.activation(qk[:, n, :], BQ[:, n * N:(n + 1) * N], ACT.Identity,
                                         bias=bcol[:, n:n + 1]).then_inc(s_qka, 1)

            def exps(g):
                act.wait_ge(s_nmx, g + 1)
                for b in range(GB):
                    for side, k in ((0, C), (1, 128)):
                        nc.scalar.activation(prob[:, b, side, 0:k], BQ[:, (2 * b + side) * 128:(2 * b + side) * 128 + k],
                                             ACT.Exp, bias=nmx[:, b, side:side + 1], scale=SCALE,
                                             accum_out=rsum[:, b, side:side + 1]).then_inc(s_e, 1)

            def pt_copy(g):
                act.wait_ge(s_pt, g + 1)
                nc.scalar.activation(pT[:].rearrange("p b s n -> p (b s n)"), BK[:], ACT.Copy).then_inc(s_pte, 1)

            def gate(g, b):
                act.wait_ge(s_av, GB * g + b + 1)
                nc.scalar.activation(gt[:, b, :], mix_bank(g, b)[:, 128:256], ACT.Tanh, scale=-0.5).then_inc(s_g, 1)

            def ht_copy(g):
                act.wait_ge(s_ht, g + 1)
                nc.scalar.activation(hT[:], BT[:, 0:N], ACT.Copy).then_inc(s_hT, 1)

            def ht_split(g):
                nc.scalar.activation(hT_hi[:], BT[:, 0:N], ACT.Copy).then_inc(s_hthi, 1)

            def silu(f, c):
                act.wait_ge(s_gu, NF * f + c + 1)
                p = 64 if c == 0 else 128
                nc.scalar.activation(sil[0:p, c % GR, :], GU[c % GR][0:p, 0:N], ACT.Silu).then_inc(s_sil, 1)

            def weights_copy(f):
                act.wait_ge(s_wtt, f + 1)
                nc.scalar.activation(wT[:], BV[:, 0:N], ACT.Copy).then_inc(s_wT, 1)

            def weights_rows(f, j, last=False):
                act.wait_ge(s_wb, (CH // 2) * f + j + 1)
                nc.scalar.activation(wbs[:, 2 * j:2 * j + 2, :].rearrange("p c n -> p (c n)"),
                                     SPREADB[j if last else 0][:],
                                     ACT.Copy).then_inc(s_wbs, 1)

            def turn(g, front=True):
                f = g - 1
                silu(f, 0)
                silu(f, 1)
                silu(f, 2)
                weights_copy(f)
                silu(f, 3)
                pt_copy(g)
                weights_rows(f, 0)
                silu(f, 4)
                gate(g, 0)
                if not front:
                    gate(g, 1)
                weights_rows(f, 1)
                silu(f, 5)
                if front:
                    gate(g, 1)
                    t_split(g + 1)
                silu(f, 6)
                weights_rows(f, 2)
                if front:
                    qk_bias(g + 1)
                silu(f, 7)
                weights_rows(f, 3)
                ht_copy(g)
                silu(f, 8)
                ht_split(g)
                if front:
                    exps(g + 1)

            act.wait_ge(s_small, 1)
            nc.scalar.activation(table_in[:], inv_e[:, 0, :], ACT.Exp)
            act.wait_ge(s_aw[0], 16)
            nc.scalar.activation(wqk_hi[:], aw[:, 0:4, :], ACT.Copy).then_inc(s_qkw, 1)
            act.wait_ge(s_t, 1)
            nc.scalar.activation(t_first[:, 0, :], BQ[:, 0:N], ACT.Copy).then_inc(s_tf, 1)
            act.wait_ge(s_tf, 2)
            nc.scalar.activation(t_hi[:].rearrange("p s n -> p (s n)"), t_first[:].rearrange("p s n -> p (s n)"),
                                 ACT.Copy).then_inc(s_thi, 1)
            act.wait_ge(s_bias, 32)
            for n in (QC, KC):
                act.wait_ge(s_qkf, n + 1)
                nc.scalar.activation(qk[:, n, :], FIRSTB[n][:, 0:N], ACT.Identity,
                                     bias=bcol[:, n:n + 1]).then_inc(s_qka, 1)

            def ffn_hi(n):
                w, hi, at = ((wsh, wsh_hi, 2), (wg, wg_hi, 0), (wu, wu_hi, 1))[n]
                act.wait_ge(s_ffn[at], 16)
                nc.scalar.activation(hi[:], w[:], ACT.Copy).then_inc(s_hi, 1)

            ffn_hi(0)
            act.wait_ge(s_wv, 3)
            nc.scalar.activation(wv_hi[:].rearrange("p s n -> p (s n)"), wv[:].rearrange("p s n -> p (s n)"),
                                 ACT.Copy).then_inc(s_wvs, 1)
            act.wait_ge(s_zero, 1)
            exps(0)
            ffn_hi(1)
            ffn_hi(2)
            pt_copy(0)
            t_split(1)
            gate(0, 0)
            gate(0, 1)
            act.wait_ge(s_cst2, 16)
            nc.scalar.activation(sel[:].rearrange("p c m -> p (c m)"), sel_f, ACT.Copy).then_inc(s_sel, 1)
            qk_bias(1)
            ht_copy(0)
            ht_split(0)
            exps(1)
            with act.Fori(1, NG - 1) as g:
                turn(g)
            turn(NG - 1, front=False)
            f = NG - 1
            silu(f, 0)
            silu(f, 1)
            silu(f, 2)
            weights_copy(f)
            silu(f, 3)
            weights_rows(f, 0, last=True)
            silu(f, 4)
            for j in range(1, CH // 2):
                weights_rows(f, j, last=True)
                silu(f, j + 4)
            silu(f, 8)

        @block.vector
        def _(dve):
            def alone(s, value):
                dve.wait_ge(s, value)
                dve.sem_inc(s_waited, 1)

            def ln1_stats(g0, g1):
                b0, b1 = g0 * GB, g1 * GB
                for b in range(b0, b1):
                    nc.vector.bn_stats(st1[:, b, :], x_all[:, b, :]).then_inc(s_st1, 1)
                for b in range(b0, b1):
                    dve.wait_ge(s_st1, b + 1)
                    nc.vector.bn_aggr(mv1[:, b, :], st1[:, b, :]).then_inc(s_mv1, 1)

            def ln1_apply(g):
                dve.wait_ge(s_rs1, g + 1)
                for b in range(GB):
                    at = g * GB + b
                    nc.vector.tensor_scalar(xn[:, b, :], x_all[:, at, :], mv1[:, at, 0:1], rs1[:, bass.ds(at, 1)],
                                            ALU.subtract, ALU.mult).then_inc(s_xn, 1)

            def t_rest(g):
                dve.wait_ge(s_thi, g + 1)
                nc.vector.tensor_tensor(t_lo[:].rearrange("p s n -> p (s n)"), BQ[:],
                                        t_hi[:].rearrange("p s n -> p (s n)").bitcast(fp32),
                                        ALU.subtract).then_inc(s_tlo, 1)

            def qk_bias(g):
                dve.wait_ge(s_qk, 2 * g + 2)
                for n in (KS, QS):
                    nc.vector.tensor_scalar(qk[:, n, :], BK[:, (n - 2) * N:(n - 1) * N], bcol[:, n:n + 1], None,
                                            ALU.add).then_inc(s_qkd, 1)

            def row_max(g):
                dve.wait_ge(s_s, g + 1)
                sc = BQ[:].rearrange("p (b s k) -> p b s k", b=GB, s=2)
                for side, k in ((0, C), (1, 128)):
                    nc.vector.tensor_reduce(mx[:, :, side], sc[:, :, side, 0:k], AX, ALU.max).then_inc(s_mx, 1)

            def neg_max(g):
                dve.wait_ge(s_mx, 2 * (g + 1))
                nc.vector.tensor_scalar(nmx[:], mx[:], -SCALE, None, ALU.mult).then_inc(s_nmx, 1)

            def values(g, b):
                dve.wait_ge(s_v, GB * g + b + 1)
                nc.vector.tensor_tensor(val[:, b, :, :].rearrange("p s n -> p (s n)"), VALB[b][:],
                                        vbias[:].rearrange("p s n -> p (s n)"), ALU.add).then_inc(s_ve, 1)

            def inverse_sum(g):
                dve.wait_ge(s_e, 4 * (g + 1))
                nc.vector.reciprocal(rinv[:], rsum[:]).then_inc(s_ri, 1)

            def normalise(g):
                dve.wait_ge(s_ri, g + 1)
                nc.vector.tensor_tensor(probn[:].rearrange("p b s k -> p (b s) k"),
                                        prob[:].rearrange("p b s k -> p (b s) k"),
                                        rinv[:].rearrange("p b s -> p (b s)").unsqueeze(2).broadcast_to([128, 2 * GB, 128]),
                                        ALU.mult).then_inc(s_pn, 1)

            def mix(g, b):
                dve.wait_ge(s_g, GB * g + b + 1)
                nc.vector.scalar_tensor_tensor(c2s[:, b, :], gt[:, b, :], 1.0, mix_bank(g, b)[:, 0:128],
                                               ALU.subtract, ALU.mult).then_inc(s_c2s, 1)
                nc.vector.scalar_tensor_tensor(s2c[:, b, :], gt[:, b, :], 1.0, mix_bank(g, b)[:, 256:384],
                                               ALU.add, ALU.mult).then_inc(s_s2c, 1)
                dve.wait_ge(s_c2s, GB * g + b + 1)
                nc.vector.tensor_tensor(xc[:, b, :], c2s[:, b, :], x_all[:, g * GB + b, :], ALU.add).then_inc(s_xc, 1)

            def mix_sum(g):
                dve.wait_ge(s_s2c, GB * (g + 1))
                dve.wait_ge(s_xc, GB * (g + 1))
                if g > 0:
                    dve.wait_ge(s_x2h, g)
                nc.vector.tensor_tensor(x2[:], s2c[:], xc[:], ALU.add).then_inc(s_x2, 1)

            def ln2_stats(g):
                dve.wait_ge(s_x2, g + 1)
                for b in range(GB):
                    nc.vector.bn_stats(st2[:, b, :], x2[:, b, :]).then_inc(s_st2, 1)
                alone(s_st2, GB * (g + 1))
                for b in range(GB):
                    nc.vector.bn_aggr(mv2[:, b, :], st2[:, b, :]).then_inc(s_mv2, 1)

            def ln2_apply(g):
                dve.wait_ge(s_rs2, g + 1)
                if not (isinstance(g, int) and g == 0):
                    dve.wait_ge(s_x2h, g)
                for b in range(GB):
                    nc.vector.tensor_scalar(h[:, b, :], x2[:, b, :], mv2[:, b, 0:1], rs2[:, b:b + 1],
                                            ALU.subtract, ALU.mult).then_inc(s_h, 1)

            def ht_rest(g):
                dve.wait_ge(s_hthi, g + 1)
                nc.vector.tensor_tensor(hT_lo[:], BT[:, 0:N], hT_hi[:].bitcast(fp32),
                                        ALU.subtract).then_inc(s_htlo, 1)

            def weigh_last(f):
                dve.wait_ge(s_wbs, (CH // 2) * (f + 1))
                dve.wait_ge(s_mul, NF * (f + 1))
                dve.wait_ge(s_d, NF * f + NF - RING)
                nc.vector.tensor_tensor(hid[:, CH % RING, :], wbs[:, CH - 1, :], mul[:, CH % RING, :],
                                        ALU.mult).then_inc(s_hidl, 1)

            def router_a(g, front=True):
                dve.wait_ge(s_rl, g + 1)
                nc.vector.tensor_tensor(lg[:], BV[:, 0:GB * E].rearrange("p (b e) -> p b e", b=GB),
                                        brow[:, 384:384 + E].unsqueeze(1).broadcast_to([128, GB, E]), ALU.add).then_inc(s_lg, 1)
                if front:
                    neg_max(g + 1)
                alone(s_lg, g + 1)
                for b in range(GB):
                    nc.vector.max(top[:, b, :], lg[:, b, :]).then_inc(s_top, 1)

            def router_top(g):
                alone(s_top, GB * (g + 1))
                for b in range(GB):
                    nc.vector.max_index(topi[:, b, :], top[:, b, :], lg[:, b, :]).then_inc(s_topi, 1)

            def up_mul(f, c):
                dve.wait_ge(s_sil, NF * f + c + 1)
                if c == 0:
                    nc.vector.tensor_tensor(hid0[0:64, :], GU[0][64:128, 0:N], sil[0:64, 0, :], ALU.mult)\
                      .then_inc(s_mul, 1)
                    return
                if c > RING:
                    dve.wait_ge(s_hid, (CH - 1) * f + c - RING)
                nc.vector.tensor_tensor(mul[:, c % RING, :], GU[c % GR][:, N:2 * N], sil[:, c % GR, :], ALU.mult)\
                  .then_inc(s_mul, 1)

            def finish(f):
                dve.wait_ge(s_d, NF * (f + 1))
                dve.wait_ge(s_x2h, f + 1)
                dve.wait_ge(s_out, 16 * (f + 1))
                nc.vector.tensor_tensor(yout[:].rearrange("p b d -> p (b d)"), Y[:, 0:N],
                                        x2h[:].rearrange("p b d -> p (b d)"), ALU.add).then_inc(s_y, 1)

            def sigmoids(g):
                dve.wait_ge(s_topi, GB * (g + 1))
                nc.vector.tensor_tensor(oh[:],
                                        iota.unsqueeze(1).unsqueeze(1).broadcast_to([128, GB, 2, E]),
                                        topi[:, :, 0:2].unsqueeze(3).broadcast_to([128, GB, 2, E]),
                                        ALU.is_equal).then_inc(s_oh, 1)
                dve.wait_ge(s_ez1, g + 1)
                nc.vector.reciprocal(sg[:], ez1[:]).then_inc(s_sg, 1)
                dve.wait_ge(s_sg, g + 1)
                nc.vector.tensor_tensor(sgs[:], sg[:, :, 0], sg[:, :, 1], ALU.add).then_inc(s_sgs, 1)

            def weights(g, front=True):
                dve.wait_ge(s_sgs, g + 1)
                nc.vector.reciprocal(sgr[:], sgs[:]).then_inc(s_sgr, 1)
                dve.wait_ge(s_sgr, g + 1)
                nc.vector.tensor_tensor(wt[:], sg[:], sgr[:].unsqueeze(2).broadcast_to([128, GB, 2]), ALU.mult).then_inc(s_wt, 1)
                if front:
                    inverse_sum(g + 1)
                dve.wait_ge(s_oh, g + 1)
                dve.wait_ge(s_wt, g + 1)
                nc.vector.tensor_tensor(ohw[:], oh[:], wt[:].unsqueeze(3).broadcast_to([128, GB, 2, E]), ALU.mult).then_inc(s_ohw, 1)

            def weights_sum(g):
                dve.wait_ge(s_ohw, g + 1)
                nc.vector.tensor_tensor(wsum[:], ohw[:, :, 0, :], ohw[:, :, 1, :], ALU.add).then_inc(s_ws, 1)
                nc.vector.tensor_tensor(wst_r[:, :, 0:E], ohw[:, :, 0, :], ohw[:, :, 1, :], ALU.add).then_inc(s_whi, 1)

            def weights_rest(g):
                dve.wait_ge(s_ws, g + 1)
                dve.wait_ge(s_whi, g + 1)
                nc.vector.tensor_tensor(wst_r[:, :, E:2 * E], wsum[:], wst[:, :, 0:E], ALU.subtract).then_inc(s_wlo, 1)

            def turn(g, front=True):
                f = g - 1
                up_mul(f, 1)
                values(g, 1)
                if front:
                    ln1_apply(g + 1)
                up_mul(f, 2)
                up_mul(f, 3)
                up_mul(f, 4)
                mix(g, 0)
                if front:
                    up_mul(f, 5)
                    mix(g, 1)
                    t_rest(g + 1)
                else:
                    mix(g, 1)
                    mix_sum(g)
                    up_mul(f, 5)
                ln2_stats(g)
                up_mul(f, 6)
                ln2_apply(g)
                if front:
                    qk_bias(g + 1)
                up_mul(f, 7)
                up_mul(f, 8)
                if front:
                    row_max(g + 1)
                router_a(g, front)
                weigh_last(f)
                ht_rest(g)
                router_top(g)
                if front:
                    values(g + 1, 0)
                sigmoids(g)
                if not front:
                    up_mul(g, 0)
                weights(g, front)
                if front:
                    up_mul(g, 0)
                weights_sum(g)
                finish(f)
                weights_rest(g)
                if front:
                    normalise(g + 1)

            nc.vector.memset(warm_up[:], 0.0).then_inc(s_warm, 1)
            dve.sem_inc(s_y, 1)
            nc.vector.memset(ctx_t[96:128, :, :], 0.0).then_inc(s_pad, 1)
            nc.vector.memset(wd[64:128, 0, :], 0.0).then_inc(s_pad, 1)
            dve.wait_ge(s_xin[0], 16)
            ln1_stats(0, 1)
            ln1_apply(0)
            dve.wait_ge(s_t, 1)
            nc.vector.tensor_copy(t_first[:, 1, :], BK[:, 0:N]).then_inc(s_tf, 1)
            dve.wait_ge(s_aw[0], 16)
            dve.wait_ge(s_qkw, 1)
            nc.vector.tensor_tensor(wqk_lo[:], aw[:, 0:4, :], wqk_hi[:].bitcast(fp32), ALU.subtract).then_inc(s_qkw, 1)
            dve.wait_ge(s_tf, 2)
            dve.wait_ge(s_thi, 1)
            nc.vector.tensor_tensor(t_lo[:], t_first[:], t_hi[:].bitcast(fp32), ALU.subtract).then_inc(s_tlo, 1)
            dve.wait_ge(s_aw[1], 16)
            nc.vector.tensor_scalar(wv[:, 0, 0:128], aw[:, 4, :], -0.5, None, ALU.mult).then_inc(s_wv, 1)
            nc.vector.tensor_scalar(wv[:, 1, 0:128], aw[:, 5, :], 0.5, None, ALU.mult).then_inc(s_wv, 1)
            dve.wait_ge(s_bias, 32)
            for n in (KS, QS):
                dve.wait_ge(s_qkf, n + 1)
                nc.vector.tensor_scalar(qk[:, n, :], FIRSTB[n][:, 0:N], bcol[:, n:n + 1], None,
                                        ALU.add).then_inc(s_qkd, 1)
            dve.wait_ge(s_prod, 1)
            nc.vector.tensor_copy(wv[:, :, 128:256], GU[2][:, 0:256].rearrange("p (s n) -> p s n", s=2)).then_inc(s_wv, 1)
            nc.vector.tensor_scalar(vbias[:, 0, 0:128], brow[:, 0:128], -0.5, None, ALU.mult).then_inc(s_vb, 1)
            nc.vector.tensor_scalar(vbias[:, 1, 0:128], brow[:, 128:256], 0.5, None, ALU.mult).then_inc(s_vb, 1)
            dve.wait_ge(s_xin[1], 16)
            ln1_stats(1, 2)
            dve.wait_ge(s_wvs, 1)
            nc.vector.tensor_tensor(wv_lo[:], wv[:], wv_hi[:].bitcast(fp32), ALU.subtract).then_inc(s_wvs, 1)
            row_max(0)
            neg_max(0)
            dve.wait_ge(s_xin[2], 16)
            ln1_stats(2, 3)
            dve.wait_ge(s_prod, 2)
            nc.vector.tensor_tensor(vbias[:, 0, 128:256], Y[:, 0:128], brow[:, 256:384], ALU.add).then_inc(s_vb, 1)
            nc.vector.tensor_copy(vbias[:, 1, 128:256], Y[:, 128:256]).then_inc(s_vb, 1)

            dve.wait_ge(s_vb, 4)
            values(0, 0)
            inverse_sum(0)
            normalise(0)
            values(0, 1)
            ln1_apply(1)
            dve.wait_ge(s_hi, 1)
            nc.vector.tensor_tensor(wsh_lo[:], wsh[:], wsh_hi[:].bitcast(fp32), ALU.subtract).then_inc(s_lo, 1)
            ln1_stats(3, 5)
            t_rest(1)
            mix(0, 0)
            mix(0, 1)
            mix_sum(0)
            ln2_stats(0)
            qk_bias(1)
            ln2_apply(0)
            ln1_stats(5, 6)
            row_max(1)
            neg_max(1)
            ht_rest(0)
            router_a(0, front=False)
            router_top(0)
            ln1_stats(6, 7)
            values(1, 0)
            dve.wait_ge(s_cst2, 16)
            sigmoids(0)
            weights(0)
            up_mul(0, 0)
            weights_sum(0)
            weights_rest(0)
            normalise(1)
            ln1_stats(7, NG)
            with dve.Fori(1, NG - 1) as g:
                turn(g)
            turn(NG - 1, front=False)
            f = NG - 1
            for c in range(1, NF):
                up_mul(f, c)
            weigh_last(f)
            finish(f)

        @block.tensor
        def _(pe):
            mm = nc.tensor.matmul

            def split3(dst, w_hi, w_lo, r_hi, r_lo):
                mm(dst, w_hi, r_hi, start=True, stop=False)
                mm(dst, w_hi, r_lo, start=False, stop=False)
                return mm(dst, w_lo, r_hi, start=False, stop=True)

            def keep_warm(n):
                for _ in range(n):
                    mm(GU[GR - 1][:, 0:128], warm_up[:], warm_up[:], start=True, stop=True)

            def transpose_in(g):
                pe.wait_ge(s_xn, GB * (g + 1))
                pe.wait_ge(s_ctx, 16 * (g + 1))
                for b in range(GB):
                    nc.tensor.transpose(BQ[:, b * 128:(b + 1) * 128], xn[:, b, :], ident)
                for b in range(GB):
                    last = nc.tensor.transpose(BQ[:, N + b * 128:N + (b + 1) * 128], ctx_t[:, b, :], ident)
                last.then_inc(s_t, 1)

            def project(g):
                pe.wait_ge(s_thi, g + 1)
                pe.wait_ge(s_tlo, g + 1)
                for n in range(4):
                    side, dst = n // 2, (BQ, BK)[n // 2][:, (n % 2) * N:(n % 2 + 1) * N]
                    last = split3(dst, wqk_hi[:, n, :], wqk_lo[:, n, :], t_hi[:, side, :], t_lo[:, side, :])
                    if n % 2:
                        last.then_inc(s_qk, 1)

            def scores(g):
                pe.wait_ge(s_qka, 2 * (g + 1))
                pe.wait_ge(s_qkd, 2 * (g + 1))
                for b in range(GB):
                    at = slice(b * 128, (b + 1) * 128)
                    mm(BQ[:, b * 256:b * 256 + C], qk[:, QC, at], qk[:, KS, b * 128:b * 128 + C], start=True, stop=True)
                    last = mm(BQ[:, b * 256 + 128:b * 256 + 256], qk[:, QS, at], qk[:, KC, at], start=True, stop=True)
                last.then_inc(s_s, 1)

            def values(g, b):
                for side in range(2):
                    at = slice(b * 128, (b + 1) * 128)
                    last = split3(VALB[b][:, side * 256:(side + 1) * 256], t_hi[:, 1 - side, at], t_lo[:, 1 - side, at],
                                  wv_hi[:, side, :], wv_lo[:, side, :])
                last.then_inc(s_v, 1)

            def probs_t(g):
                pe.wait_ge(s_pn, g + 1)
                pe.wait_ge(s_ve, GB * g + 1)
                for b in range(GB):
                    nc.tensor.transpose(BK[:, b * 256:b * 256 + 128], probn[:, b, 0, :], ident)
                    last = mm(BK[:, b * 256 + 128:b * 256 + 256], probn[0:C, b, 1, :], interpT[0:C, :],
                              start=True, stop=True)
                last.then_inc(s_pt, 1)

            def mix(g, b):
                if b == 0:
                    pe.wait_ge(s_pte, g + 1)
                    pe.wait_ge(s_ve, GB * (g + 1))
                elif not isinstance(g, int):
                    pe.wait_ge(s_wbs, (CH // 2) * (g - 1) + 2)
                mm(mix_bank(g, b)[:, 0:256], pT[0:C, b, 0, :], val[0:C, b, 0, :], start=True, stop=False, skip_group_check=True)
                mm(mix_bank(g, b)[:, 128:256], pT[:, b, 1, :], val[:, b, 1, 128:256], start=False, stop=True,
                   skip_group_check=True)
                mm(mix_bank(g, b)[:, 256:384], pT[:, b, 1, :], val[:, b, 1, 0:128], start=False, stop=True,
                   skip_group_check=True).then_inc(s_av, 1)

            def transpose_h(g):
                pe.wait_ge(s_h, GB * (g + 1))
                for b in range(GB):
                    last = nc.tensor.transpose(BT[:, b * 128:(b + 1) * 128], h[:, b, :], ident)
                last.then_inc(s_ht, 1)

            def logits(g):
                pe.wait_ge(s_hT, g + 1)
                if not (isinstance(g, int) and g == 0):
                    pe.wait_ge(s_wbs, (CH // 2) * g)
                for b in range(GB):
                    last = mm(BV[:, b * E:(b + 1) * E], hT[:, b * 128:(b + 1) * 128], gate_w[:], start=True, stop=True)
                last.then_inc(s_rl, 1)

            def weights_t(f):
                pe.wait_ge(s_wlo, f + 1)
                for b in range(GB):
                    last = nc.tensor.transpose(BV[:, b * 128:(b + 1) * 128], wst[:, b, :], ident)
                last.then_inc(s_wtt, 1)

            def gate_up(f, c):
                if c == 0:
                    pe.wait_ge(s_hthi, f + 1)
                    pe.wait_ge(s_htlo, f + 1)
                if c >= GR:
                    pe.wait_ge(s_mul, NF * f + c - GR + 1)
                if c == 0:
                    split3(GU[0][:, 0:N], wsh_hi[:], wsh_lo[:], hT_hi[:], hT_lo[:]).then_inc(s_gu, 1)
                    return
                at = slice((c - 1) * 128, c * 128)
                split3(GU[c % GR][:, 0:N], wg_hi[:, at], wg_lo[:, at], hT_hi[:], hT_lo[:])
                split3(GU[c % GR][:, N:2 * N], wu_hi[:, at], wu_lo[:, at], hT_hi[:], hT_lo[:]).then_inc(s_gu, 1)

            def spread(f, j, last=False):
                if j == 0:
                    pe.wait_ge(s_wT, f + 1)
                elif not last:
                    pe.wait_ge(s_wbs, (CH // 2) * f + j)
                if j == 2 and not last:
                    pe.wait_ge(s_xc, GB * (f + 2))
                for i in range(2):
                    prod = mm(SPREADB[j if last else 0][:, i * N:(i + 1) * N], sel[:, 2 * j + i, :], wT[:], start=True, stop=True)
                prod.then_inc(s_wb, 1)

            def down(f, c):
                if c == 0:
                    pe.wait_ge(s_mul, NF * f + 1)
                    pe.wait_ge(s_y, f + 1)
                elif c == CH:
                    pe.wait_ge(s_hidl, f + 1)
                else:
                    pe.wait_ge(s_hid, (CH - 1) * f + c)
                src = hid0[:] if c == 0 else hid[:, c % RING, :]
                for b in range(GB):
                    last = mm(Y[:, b * 128:(b + 1) * 128], src[:, b * 128:(b + 1) * 128], wd[:, c, :],
                              start=(c == 0 and b == 0), stop=(c == NF - 1), skip_group_check=True)
                last.then_inc(s_d, 1)

            def turn(g, front=True):
                f = g - 1
                gate_up(f, 0)
                gate_up(f, 1)
                values(g, 1)
                gate_up(f, 2)
                gate_up(f, 3)
                weights_t(f)
                down(f, 0)
                probs_t(g)
                spread(f, 0)
                gate_up(f, 4)
                mix(g, 0)
                if front:
                    spread(f, 1)
                    gate_up(f, 5)
                    down(f, 1)
                    mix(g, 1)
                    transpose_in(g + 1)
                else:
                    mix(g, 1)
                    spread(f, 1)
                    gate_up(f, 5)
                    down(f, 1)
                down(f, 2)
                gate_up(f, 6)
                spread(f, 2)
                down(f, 3)
                if front:
                    project(g + 1)
                gate_up(f, 7)
                down(f, 4)
                spread(f, 3)
                transpose_h(g)
                gate_up(f, 8)
                if front:
                    scores(g + 1)
                logits(g)
                for c in range(5, NF - 1):
                    down(f, c)
                if front:
                    values(g + 1, 0)
                down(f, NF - 1)

            pe.wait_ge(s_warm, 1)
            keep_warm(WARM_UP)
            pe.wait_ge(s_cst, 16)
            pe.wait_ge(s_pad, 2)
            pe.wait_ge(s_ctx, 16)
            for b in range(GB):
                nc.tensor.transpose(BK[:, b * 128:(b + 1) * 128], ctx_t[:, b, :], ident)
            pe.wait_ge(s_xn, GB)
            for b in range(GB):
                last = nc.tensor.transpose(BQ[:, b * 128:(b + 1) * 128], xn[:, b, :], ident)
            last.then_inc(s_t, 1)
            pe.wait_ge(s_aw[0], 16)
            pe.wait_ge(s_tf, 2)
            pe.sem_inc(s_qk, 2)
            for n in range(4):
                mm(FIRSTB[n][:, 0:N], aw[:, n, :], t_first[:, n // 2, :], start=True, stop=True).then_inc(s_qkf, 1)
            pe.wait_ge(s_aw[1], 16)
            pe.wait_ge(s_bias, 32)
            for side in range(2):
                last = mm(GU[2][:, side * 128:(side + 1) * 128], aw[:, 6 + side, :], aw[:, 8 + side, :], start=True, stop=True)
            last.then_inc(s_prod, 1)
            scores(0)
            for side in range(2):
                last = mm(Y[:, side * 128:(side + 1) * 128], bcol[:, 4 + side:5 + side].broadcast_to([128, 128]),
                          aw[:, 8 + side, :], start=True, stop=True)
            last.then_inc(s_prod, 1)
            pe.wait_ge(s_wvs, 2)
            pe.wait_ge(s_thi, 1)
            pe.wait_ge(s_tlo, 1)
            values(0, 0)
            values(0, 1)
            keep_warm(BRIDGES[0])
            probs_t(0)
            keep_warm(BRIDGES[1])
            transpose_in(1)
            mix(0, 0)
            mix(0, 1)
            pe.wait_ge(s_qkw, 2)
            project(1)
            keep_warm(BRIDGES[2])
            scores(1)
            transpose_h(0)
            pe.wait_ge(s_ffn[3], 48)
            logits(0)
            values(1, 0)
            pe.wait_ge(s_lo, 3)
            pe.wait_ge(s_sel, 1)
            pe.wait_ge(s_vb, 4)
            with pe.Fori(1, NG - 1) as g:
                turn(g)
            turn(NG - 1, front=False)
            f = NG - 1
            gate_up(f, 0)
            gate_up(f, 1)
            gate_up(f, 2)
            gate_up(f, 3)
            weights_t(f)
            down(f, 0)
            spread(f, 0, last=True)
            gate_up(f, 4)
            for j in range(1, CH // 2):
                spread(f, j, last=True)
            gate_up(f, 5)
            for c in range(6, NF):
                down(f, c - 5)
                gate_up(f, c)
            for c in range(NF - 5, NF):
                down(f, c)


def kernel(x, ctx_1024, L0_xattn_Wq_c, L0_xattn_bq_c, L0_xattn_Wk_s, L0_xattn_bk_s, L0_xattn_Wv_s, L0_xattn_bv_s,
           L0_xattn_Wq_s, L0_xattn_bq_s, L0_xattn_Wk_c, L0_xattn_bk_c, L0_xattn_Wv_c, L0_xattn_bv_c, L0_xattn_Wg,
           L0_xattn_bg, L0_ffn_gate_w, L0_ffn_gate_b, L0_ffn_shared_wg, L0_ffn_shared_wu, L0_ffn_shared_wd,
           L0_ffn_experts_wg, L0_ffn_experts_wu, L0_ffn_experts_wd):
    import numpy as np
    import concourse.bacc as bacc
    from concourse.bass_utils import run_bass_kernel_spmd

    def arr(a):
        return np.ascontiguousarray(a)

    x, ctx_1024 = arr(x), arr(ctx_1024)
    D, C = x.shape[2], ctx_1024.shape[1]
    T = x.shape[1]
    E = L0_ffn_gate_w.shape[1]
    H = L0_ffn_shared_wg.shape[1]
    wg_gate = arr(L0_xattn_Wg)
    attn_w = arr(np.concatenate([arr(L0_xattn_Wq_c).T, arr(L0_xattn_Wk_c).T, arr(L0_xattn_Wk_s).T, arr(L0_xattn_Wq_s).T,
                                 arr(L0_xattn_Wv_s).T, arr(L0_xattn_Wv_c).T, arr(L0_xattn_Wv_s), arr(L0_xattn_Wv_c),
                                 wg_gate[:, :D].T, wg_gate[:, D:].T], axis=1))
    bias_col = arr(np.stack([arr(b) for b in (L0_xattn_bq_c, L0_xattn_bk_c, L0_xattn_bk_s, L0_xattn_bq_s,
                                              L0_xattn_bv_s, L0_xattn_bv_c)], axis=1))
    bias_row = arr(np.concatenate([arr(L0_xattn_bv_s), arr(L0_xattn_bv_c), arr(L0_xattn_bg), arr(L0_ffn_gate_b)]))
    wg = arr(np.transpose(arr(L0_ffn_experts_wg), (1, 0, 2)).reshape(D, E * H))
    wu = arr(np.transpose(arr(L0_ffn_experts_wu), (1, 0, 2)).reshape(D, E * H))
    wsh = arr(np.concatenate([arr(L0_ffn_shared_wg), arr(L0_ffn_shared_wu), arr(L0_ffn_gate_w)], axis=1))
    wd = arr(np.concatenate([arr(L0_ffn_shared_wd), arr(L0_ffn_experts_wd).reshape(E * H, D)], axis=0))

    consts = np.zeros((128, 256 + (E * H // 128) * 128 + E), np.float32)
    consts[:, 0:128] = np.eye(128, dtype=np.float32)
    pos = np.clip((np.arange(T, dtype=np.float32) + np.float32(0.5)) * np.float32(C / T) - np.float32(0.5), 0, C - 1)
    lo = np.floor(pos).astype(np.int32)
    for t in range(T):
        w = pos[t] - np.float32(lo[t])
        consts[lo[t], 128 + t] += 1 - w
        consts[min(lo[t] + 1, C - 1), 128 + t] += w
    for c in range(E * H // 128):
        for m in range(128):
            e = (128 * c + m) // H
            consts[e, 256 + 128 * c + m] = 1
            consts[E + e, 256 + 128 * c + m] = 1
    consts[:, -E:] = np.arange(E, dtype=np.float32)

    arrays = dict(x=x, ctx_in=ctx_1024, attn_w=attn_w, bias_col=bias_col, bias_row=bias_row, const_in=consts,
                  wg_in=wg, wu_in=wu, wsh_in=wsh, wd_in=wd)
    nc = bacc.Bacc("TRN2", target_bir_lowering=False, num_devices=1)
    args = [nc.dram_tensor(name, a.shape, mybir.dt.from_np(a.dtype), kind="ExternalInput").ap()
            for name, a in arrays.items()]
    out = nc.dram_tensor("out", x.shape, mybir.dt.float32, kind="ExternalOutput").ap()
    xattn_ffn_kernel(nc, *args, out)
    return run_bass_kernel_spmd(nc, [arrays], core_ids=[0]).results[0]["out"]
```
